# Optimizing a Trainium2 kernel written in Bass

```python
import numpy as np
import jax
import jax.numpy as jnp

def _softmax(x, axis=-1):
    return jax.nn.softmax(x, axis=axis)

def _gelu(x):
    return jax.nn.gelu(x, approximate=True)

def _silu(x):
    return jax.nn.silu(x)

def _sigmoid(x):
    return jax.nn.sigmoid(x)

def _layernorm(x, axis=-1, eps=1e-05):
    m = jnp.mean(x, axis=axis, keepdims=True)
    v = jnp.var(x, axis=axis, keepdims=True)
    return (x - m) / jnp.sqrt(v + eps)

def _scatter_add(tgt, idx, src, axis=0):
    return tgt.at[idx].add(src)

def _segment_sum(src, seg, n):
    return jax.ops.segment_sum(src, seg, n)
kernel_name = 'mk_pixart_resid_d2_seqx_r4_c164ea'

def setup_inputs(seed: int=0):
    np.random.seed(seed)
    _w = jnp.asarray

    def _rec_inputs():
        import jax
        import jax.numpy as jnp
        _rk = jax.random.key(seed)
        x = -0.0002928 + 1 * jax.random.normal(jax.random.fold_in(_rk, 1), (16, 112, 256), jnp.float32)
        _lenS = 112 - jax.random.randint(jax.random.fold_in(_rk, 7), (16,), 0, max(1, 112 // 4) + 1, jnp.int32)
        _lenS2 = 375 - jax.random.randint(jax.random.fold_in(_rk, 8), (16,), 0, max(1, 375 // 4) + 1, jnp.int32)
        cond_1024 = 0.000887014 + 1.03683 * jax.random.normal(jax.random.fold_in(_rk, 11), (16, 256), jnp.float32)
        _ctx_1024P = jax.random.normal(jax.random.fold_in(_rk, 12), (16, 16, 256), jnp.float32)
        _ctx_1024c = jax.random.dirichlet(jax.random.fold_in(_rk, 512), 0.3 * jnp.ones((16,), jnp.float32), (16, 375))
        _ctx_1024t = jnp.einsum('bsk,bkd->bsd', _ctx_1024c, _ctx_1024P)
        _ctx_1024t = _ctx_1024t * jax.lax.rsqrt(jnp.mean(jnp.square(_ctx_1024t)) + 1e-12) * 0.953939
        ctx_1024 = -0.000761806 + 0.999296 * (_ctx_1024t + 0.3 * jax.random.normal(jax.random.fold_in(_rk, 612), (16, 375, 256), jnp.float32))
        return (x, cond_1024, ctx_1024)
    x, cond_1024, ctx_1024 = _rec_inputs()

    def _L0_xcond_setup():
        import jax, jax.numpy as jnp
        import numpy as np
        import math
        B, S, CTX, D, H, DH = (2, 512, 64, 256, 16, 64)
        INNER = H * DH
        DFF = 4 * D

        def layernorm(x, eps=1e-05):
            m = jnp.mean(x, axis=-1, keepdims=True)
            v = jnp.var(x, axis=-1, keepdims=True)
            return (x - m) * jax.lax.rsqrt(v + eps)

        def adaln(x, t, w, b):
            emb = t @ w + b
            scale, shift = jnp.split(emb, 2, axis=-1)
            return layernorm(x) * (1.0 + scale) + shift

        def mha(xq, ctx, wq, wk, wv, wo, bo):
            b, sq, _ = xq.shape
            sk = ctx.shape[1]
            q = (xq @ wq).reshape(b, sq, H, DH).transpose(0, 2, 1, 3)
            k = (ctx @ wk).reshape(b, sk, H, DH).transpose(0, 2, 1, 3)
            v = (ctx @ wv).reshape(b, sk, H, DH).transpose(0, 2, 1, 3)
            scores = jnp.einsum('bhqd,bhkd->bhqk', q, k) / math.sqrt(DH)
            attn = jax.nn.softmax(scores, axis=-1)
            out = jnp.einsum('bhqk,bhkd->bhqd', attn, v)
            out = out.transpose(0, 2, 1, 3).reshape(b, sq, INNER)
            return out @ wo + bo

        def glu_ff(x, w1, b1, w2, b2):
            u = x @ w1 + b1
            a, gate = jnp.split(u, 2, axis=-1)
            return a * jax.nn.gelu(gate, approximate=False) @ w2 + b2
        key = jax.random.key(seed)
        ks = jax.random.split(key, 24)
        s = 1.0 / math.sqrt(D)

        def n(k, shape, scale=1.0):
            return jax.random.normal(k, shape, dtype=jnp.float32) * scale
        return {'x': n(ks[0], (B, S, D)), 't': n(ks[1], (B, 1, D)), 'context': n(ks[2], (B, CTX, D)), 'attn1_wq': n(ks[3], (D, INNER), s), 'attn1_wk': n(ks[4], (D, INNER), s), 'attn1_wv': n(ks[5], (D, INNER), s), 'attn1_wo': n(ks[6], (INNER, D), s), 'attn1_bo': n(ks[7], (D,), 0.01), 'attn2_wq': n(ks[8], (D, INNER), s), 'attn2_wk': n(ks[9], (D, INNER), s), 'attn2_wv': n(ks[10], (D, INNER), s), 'attn2_wo': n(ks[11], (INNER, D), s), 'attn2_bo': n(ks[12], (D,), 0.01), 'ff_w1': n(ks[13], (D, 2 * DFF), s), 'ff_b1': n(ks[14], (2 * DFF,), 0.01), 'ff_w2': n(ks[15], (DFF, D), 1.0 / math.sqrt(DFF)), 'ff_b2': n(ks[16], (D,), 0.01), 'norm1_w': n(ks[17], (D, 2 * D), s), 'norm1_b': n(ks[18], (2 * D,), 0.01), 'norm2_w': n(ks[19], (D, 2 * D), s), 'norm2_b': n(ks[20], (2 * D,), 0.01), 'norm3_w': n(ks[21], (D, 2 * D), s), 'norm3_b': n(ks[22], (2 * D,), 0.01)}
    _L0_xcond_all = _L0_xcond_setup()
    _L0_xcond_in = {k: v for k, v in _L0_xcond_all.items() if k in ('attn1_wq', 'attn1_wk', 'attn1_wv', 'attn1_wo', 'attn1_bo', 'attn2_wq', 'attn2_wk', 'attn2_wv', 'attn2_wo', 'attn2_bo', 'ff_w1', 'ff_b1', 'ff_w2', 'ff_b2', 'norm1_w', 'norm1_b', 'norm2_w', 'norm2_b', 'norm3_w', 'norm3_b')}
    del _L0_xcond_all

    def _L0_ffn_setup():
        import jax, jax.numpy as jnp
        import numpy as np
        B, S, H, I, E, K = (2, 128, 256, 128, 64, 8)
        key = jax.random.key(seed)
        ks = jax.random.split(key, 8)
        return {'hidden_states': jax.random.normal(ks[0], (B, S, H), dtype=jnp.float32), 'router_w': jax.random.normal(ks[1], (H, E), dtype=jnp.float32) * 0.02, 'shared_gate_w': jax.random.normal(ks[2], (H, I), dtype=jnp.float32) * 0.02, 'shared_up_w': jax.random.normal(ks[3], (H, I), dtype=jnp.float32) * 0.02, 'shared_down_w': jax.random.normal(ks[4], (I, H), dtype=jnp.float32) * 0.02, 'expert_gate_k': jax.random.normal(ks[5], (E, H, I), dtype=jnp.float32) * 0.02, 'expert_up_k': jax.random.normal(ks[6], (E, H, I), dtype=jnp.float32) * 0.02, 'expert_down_k': jax.random.normal(ks[7], (E, I, H), dtype=jnp.float32) * 0.02}
    _L0_ffn_all = _L0_ffn_setup()
    _L0_ffn_in = {k: v for k, v in _L0_ffn_all.items() if k in ('router_w', 'shared_gate_w', 'shared_up_w', 'shared_down_w', 'expert_gate_k', 'expert_up_k', 'expert_down_k')}
    del _L0_ffn_all

    def _L1_xcond_setup():
        import jax, jax.numpy as jnp
        import numpy as np
        DIM = 256
        DIM_HEAD = 64
        HEADS = 16
        INNER = DIM_HEAD * HEADS
        B, N1, N2 = (8, 1024, 64)
        EPS = 1e-05

        def layer_norm(x, w, b):
            mu = jnp.mean(x, axis=-1, keepdims=True)
            var = jnp.var(x, axis=-1, keepdims=True)
            return (x - mu) * jax.lax.rsqrt(var + EPS) * w + b
        key = jax.random.key(seed)
        ks = jax.random.split(key, 10)
        return {'x': jax.random.normal(ks[0], (B, N1, DIM), jnp.float32), 'latents': jax.random.normal(ks[1], (B, N2, DIM), jnp.float32), 'shift': jax.random.normal(ks[2], (B, DIM), jnp.float32), 'scale': jax.random.normal(ks[3], (B, DIM), jnp.float32), 'ln1_w': jnp.ones((DIM,), jnp.float32), 'ln1_b': jnp.zeros((DIM,), jnp.float32), 'ln2_w': jnp.ones((DIM,), jnp.float32), 'ln2_b': jnp.zeros((DIM,), jnp.float32), 'Wq': jax.random.normal(ks[4], (INNER, DIM), jnp.float32) * 0.02, 'Wkv': jax.random.normal(ks[5], (2 * INNER, DIM), jnp.float32) * 0.02, 'Wo': jax.random.normal(ks[6], (DIM, INNER), jnp.float32) * 0.02}
    _L1_xcond_all = _L1_xcond_setup()
    _L1_xcond_in = {k: v for k, v in _L1_xcond_all.items() if k in ('ln1_w', 'ln1_b', 'ln2_w', 'ln2_b', 'Wq', 'Wkv', 'Wo')}
    del _L1_xcond_all

    def _L1_ffn_setup():
        import jax, jax.numpy as jnp
        import numpy as np
        B, S, D, F, E = (4, 512, 256, 1024, 8)
        key = jax.random.key(seed)
        ks = jax.random.split(key, 7)
        s1 = 1.0 / np.sqrt(D)
        s2 = 1.0 / np.sqrt(F)
        x = jax.random.normal(ks[0], (B, S, D), dtype=jnp.float32)
        W1 = jax.random.uniform(ks[1], (E, D, F), jnp.float32, -s1, s1)
        b1 = jax.random.uniform(ks[2], (E, F), jnp.float32, -s1, s1)
        W2 = jax.random.uniform(ks[3], (E, F, D), jnp.float32, -s2, s2)
        b2 = jax.random.uniform(ks[4], (E, D), jnp.float32, -s2, s2)
        Wr = jax.random.uniform(ks[5], (D, E), jnp.float32, -s1, s1)
        br = jax.random.uniform(ks[6], (E,), jnp.float32, -s1, s1)
        return {'x': x, 'W1': W1, 'b1': b1, 'W2': W2, 'b2': b2, 'Wr': Wr, 'br': br}
    _L1_ffn_all = _L1_ffn_setup()
    _L1_ffn_in = {k: v for k, v in _L1_ffn_all.items() if k in ('W1', 'b1', 'W2', 'b2', 'Wr', 'br')}
    del _L1_ffn_all
    return {'x': x, 'cond_1024': cond_1024, 'ctx_1024': ctx_1024, 'L0_xcond_attn1_wq': _L0_xcond_in['attn1_wq'], 'L0_xcond_attn1_wk': _L0_xcond_in['attn1_wk'], 'L0_xcond_attn1_wv': _L0_xcond_in['attn1_wv'], 'L0_xcond_attn1_wo': _L0_xcond_in['attn1_wo'], 'L0_xcond_attn1_bo': _L0_xcond_in['attn1_bo'], 'L0_xcond_attn2_wq': _L0_xcond_in['attn2_wq'], 'L0_xcond_attn2_wk': _L0_xcond_in['attn2_wk'], 'L0_xcond_attn2_wv': _L0_xcond_in['attn2_wv'], 'L0_xcond_attn2_wo': _L0_xcond_in['attn2_wo'], 'L0_xcond_attn2_bo': _L0_xcond_in['attn2_bo'], 'L0_xcond_ff_w1': _L0_xcond_in['ff_w1'], 'L0_xcond_ff_b1': _L0_xcond_in['ff_b1'], 'L0_xcond_ff_w2': _L0_xcond_in['ff_w2'], 'L0_xcond_ff_b2': _L0_xcond_in['ff_b2'], 'L0_xcond_norm1_w': _L0_xcond_in['norm1_w'], 'L0_xcond_norm1_b': _L0_xcond_in['norm1_b'], 'L0_xcond_norm2_w': _L0_xcond_in['norm2_w'], 'L0_xcond_norm2_b': _L0_xcond_in['norm2_b'], 'L0_xcond_norm3_w': _L0_xcond_in['norm3_w'], 'L0_xcond_norm3_b': _L0_xcond_in['norm3_b'], 'L0_ffn_router_w': _L0_ffn_in['router_w'], 'L0_ffn_shared_gate_w': _L0_ffn_in['shared_gate_w'], 'L0_ffn_shared_up_w': _L0_ffn_in['shared_up_w'], 'L0_ffn_shared_down_w': _L0_ffn_in['shared_down_w'], 'L0_ffn_expert_gate_k': _L0_ffn_in['expert_gate_k'], 'L0_ffn_expert_up_k': _L0_ffn_in['expert_up_k'], 'L0_ffn_expert_down_k': _L0_ffn_in['expert_down_k'], 'L1_xcond_ln1_w': _L1_xcond_in['ln1_w'], 'L1_xcond_ln1_b': _L1_xcond_in['ln1_b'], 'L1_xcond_ln2_w': _L1_xcond_in['ln2_w'], 'L1_xcond_ln2_b': _L1_xcond_in['ln2_b'], 'L1_xcond_Wq': _L1_xcond_in['Wq'], 'L1_xcond_Wkv': _L1_xcond_in['Wkv'], 'L1_xcond_Wo': _L1_xcond_in['Wo'], 'L1_ffn_W1': _L1_ffn_in['W1'], 'L1_ffn_b1': _L1_ffn_in['b1'], 'L1_ffn_W2': _L1_ffn_in['W2'], 'L1_ffn_b2': _L1_ffn_in['b2'], 'L1_ffn_Wr': _L1_ffn_in['Wr'], 'L1_ffn_br': _L1_ffn_in['br']}

def reference(x, cond_1024, ctx_1024, L0_xcond_attn1_wq, L0_xcond_attn1_wk, L0_xcond_attn1_wv, L0_xcond_attn1_wo, L0_xcond_attn1_bo, L0_xcond_attn2_wq, L0_xcond_attn2_wk, L0_xcond_attn2_wv, L0_xcond_attn2_wo, L0_xcond_attn2_bo, L0_xcond_ff_w1, L0_xcond_ff_b1, L0_xcond_ff_w2, L0_xcond_ff_b2, L0_xcond_norm1_w, L0_xcond_norm1_b, L0_xcond_norm2_w, L0_xcond_norm2_b, L0_xcond_norm3_w, L0_xcond_norm3_b, L0_ffn_router_w, L0_ffn_shared_gate_w, L0_ffn_shared_up_w, L0_ffn_shared_down_w, L0_ffn_expert_gate_k, L0_ffn_expert_up_k, L0_ffn_expert_down_k, L1_xcond_ln1_w, L1_xcond_ln1_b, L1_xcond_ln2_w, L1_xcond_ln2_b, L1_xcond_Wq, L1_xcond_Wkv, L1_xcond_Wo, L1_ffn_W1, L1_ffn_b1, L1_ffn_W2, L1_ffn_b2, L1_ffn_Wr, L1_ffn_br):
    import jax
    import jax.numpy as jnp

    def _L0_xcond_ref(x, t, context, attn1_wq, attn1_wk, attn1_wv, attn1_wo, attn1_bo, attn2_wq, attn2_wk, attn2_wv, attn2_wo, attn2_bo, ff_w1, ff_b1, ff_w2, ff_b2, norm1_w, norm1_b, norm2_w, norm2_b, norm3_w, norm3_b):
        import jax, jax.numpy as jnp
        import numpy as np
        import math
        B, S, CTX, D, H, DH = (2, 512, 64, 256, 16, 64)
        INNER = H * DH
        DFF = 4 * D

        def layernorm(x, eps=1e-05):
            m = jnp.mean(x, axis=-1, keepdims=True)
            v = jnp.var(x, axis=-1, keepdims=True)
            return (x - m) * jax.lax.rsqrt(v + eps)

        def adaln(x, t, w, b):
            emb = t @ w + b
            scale, shift = jnp.split(emb, 2, axis=-1)
            return layernorm(x) * (1.0 + scale) + shift

        def mha(xq, ctx, wq, wk, wv, wo, bo):
            b, sq, _ = xq.shape
            sk = ctx.shape[1]
            q = (xq @ wq).reshape(b, sq, H, DH).transpose(0, 2, 1, 3)
            k = (ctx @ wk).reshape(b, sk, H, DH).transpose(0, 2, 1, 3)
            v = (ctx @ wv).reshape(b, sk, H, DH).transpose(0, 2, 1, 3)
            scores = jnp.einsum('bhqd,bhkd->bhqk', q, k) / math.sqrt(DH)
            attn = jax.nn.softmax(scores, axis=-1)
            out = jnp.einsum('bhqk,bhkd->bhqd', attn, v)
            out = out.transpose(0, 2, 1, 3).reshape(b, sq, INNER)
            return out @ wo + bo

        def glu_ff(x, w1, b1, w2, b2):
            u = x @ w1 + b1
            a, gate = jnp.split(u, 2, axis=-1)
            return a * jax.nn.gelu(gate, approximate=False) @ w2 + b2
        h1 = adaln(x, t, norm1_w, norm1_b)
        x = mha(h1, h1, attn1_wq, attn1_wk, attn1_wv, attn1_wo, attn1_bo) + x
        h2 = adaln(x, t, norm2_w, norm2_b)
        x = mha(h2, context, attn2_wq, attn2_wk, attn2_wv, attn2_wo, attn2_bo) + x
        h3 = adaln(x, t, norm3_w, norm3_b)
        x = glu_ff(h3, ff_w1, ff_b1, ff_w2, ff_b2) + x
        return x

    def _L0_ffn_ref(hidden_states, router_w, shared_gate_w, shared_up_w, shared_down_w, expert_gate_k, expert_up_k, expert_down_k):
        import jax, jax.numpy as jnp
        import numpy as np
        B, S, H, I, E, K = (2, 128, 256, 128, 64, 8)
        logits = jnp.einsum('bsh,he->bse', hidden_states.astype(jnp.float32), router_w)
        affinity = jax.nn.sigmoid(logits)
        top_scores, top_idx = jax.lax.top_k(affinity, K)
        top_w = top_scores / (jnp.sum(top_scores, axis=-1, keepdims=True) + 1e-09)
        one_hot = jax.nn.one_hot(top_idx, E, dtype=top_w.dtype)
        router_mask = jnp.einsum('bske,bsk->bse', one_hot, top_w).astype(hidden_states.dtype)
        shared = jnp.einsum('bsi,ih->bsh', jax.nn.silu(hidden_states @ shared_gate_w) * (hidden_states @ shared_up_w), shared_down_w)
        gate_out = jnp.einsum('bsh,ehi->bsei', hidden_states, expert_gate_k)
        up_out = jnp.einsum('bsh,ehi->bsei', hidden_states, expert_up_k)
        expert_act = jax.nn.silu(gate_out) * up_out
        routed = jnp.einsum('bsei,eih->bsh', expert_act * router_mask[..., None], expert_down_k)
        return shared + routed

    def _L1_xcond_ref(x, latents, shift, scale, ln1_w, ln1_b, ln2_w, ln2_b, Wq, Wkv, Wo):
        import jax, jax.numpy as jnp
        import numpy as np
        DIM = 256
        DIM_HEAD = 64
        HEADS = 16
        INNER = DIM_HEAD * HEADS
        B, N1, N2 = (8, 1024, 64)
        EPS = 1e-05

        def layer_norm(x, w, b):
            mu = jnp.mean(x, axis=-1, keepdims=True)
            var = jnp.var(x, axis=-1, keepdims=True)
            return (x - mu) * jax.lax.rsqrt(var + EPS) * w + b
        x = layer_norm(x, ln1_w, ln1_b)
        lat = layer_norm(latents, ln2_w, ln2_b)
        lat = lat * (1.0 + scale[:, None, :]) + shift[:, None, :]
        b, n2, _ = lat.shape
        q = jnp.einsum('bld,ed->ble', lat, Wq)
        kv_in = jnp.concatenate((x, lat), axis=-2)
        kv = jnp.einsum('bld,ed->ble', kv_in, Wkv)
        k, v = jnp.split(kv, 2, axis=-1)

        def to_heads(t):
            bsz, L, _ = t.shape
            return t.reshape(bsz, L, HEADS, DIM_HEAD).transpose(0, 2, 1, 3)
        q, k, v = (to_heads(q), to_heads(k), to_heads(v))
        attn_scale = 1.0 / np.sqrt(np.sqrt(DIM_HEAD)).astype(np.float32)
        logits = jnp.einsum('bhqd,bhkd->bhqk', q * attn_scale, k * attn_scale)
        w = jax.nn.softmax(logits.astype(jnp.float32), axis=-1).astype(logits.dtype)
        out = jnp.einsum('bhqk,bhkd->bhqd', w, v)
        out = out.transpose(0, 2, 1, 3).reshape(b, n2, INNER)
        return jnp.einsum('ble,de->bld', out, Wo)

    def _L1_ffn_ref(x, W1, b1, W2, b2, Wr, br):
        import jax, jax.numpy as jnp
        import numpy as np
        B, S, D, F, E = (4, 512, 256, 1024, 8)
        b, s, d = x.shape
        e = Wr.shape[1]
        logits = x @ Wr + br
        idx = jnp.argmax(logits, axis=-1)
        probs = jax.nn.softmax(logits, axis=-1)
        gates = jnp.take_along_axis(probs, idx[..., None], axis=-1)[..., 0]
        xf = x.reshape(-1, d)
        idxf = idx.reshape(-1)
        gf = gates.reshape(-1)
        out = jnp.zeros_like(xf)
        for ei in range(e):
            h = jax.nn.gelu(xf @ W1[ei] + b1[ei], approximate=False)
            y = h @ W2[ei] + b2[ei]
            mask = (idxf == ei).astype(xf.dtype)
            out = out + y * (gf * mask)[:, None]
        return out.reshape(b, s, d)
    x = x + _L0_xcond_ref(_layernorm(x, axis=-1), cond_1024[:, None, :], ctx_1024, L0_xcond_attn1_wq, L0_xcond_attn1_wk, L0_xcond_attn1_wv, L0_xcond_attn1_wo, L0_xcond_attn1_bo, L0_xcond_attn2_wq, L0_xcond_attn2_wk, L0_xcond_attn2_wv, L0_xcond_attn2_wo, L0_xcond_attn2_bo, L0_xcond_ff_w1, L0_xcond_ff_b1, L0_xcond_ff_w2, L0_xcond_ff_b2, L0_xcond_norm1_w, L0_xcond_norm1_b, L0_xcond_norm2_w, L0_xcond_norm2_b, L0_xcond_norm3_w, L0_xcond_norm3_b)
    x = x + _L0_ffn_ref(_layernorm(x, axis=-1), L0_ffn_router_w, L0_ffn_shared_gate_w, L0_ffn_shared_up_w, L0_ffn_shared_down_w, L0_ffn_expert_gate_k, L0_ffn_expert_up_k, L0_ffn_expert_down_k)
    x = x + _L1_xcond_ref(ctx_1024, _layernorm(x, axis=-1), cond_1024, cond_1024, L1_xcond_ln1_w, L1_xcond_ln1_b, L1_xcond_ln2_w, L1_xcond_ln2_b, L1_xcond_Wq, L1_xcond_Wkv, L1_xcond_Wo)
    x = x + _L1_ffn_ref(_layernorm(x, axis=-1), L1_ffn_W1, L1_ffn_b1, L1_ffn_W2, L1_ffn_b2, L1_ffn_Wr, L1_ffn_br)
    return x

_drawn_inputs = setup_inputs


def setup_inputs(seed=0):
    import zlib

    import numpy as np

    out = dict(_drawn_inputs(seed))
    spreads = {'L1_xcond_ln1_w': (1.0, 0.6),
     'L1_xcond_ln1_b': (0.0, 0.8),
     'L1_xcond_ln2_w': (1.0, 0.6),
     'L1_xcond_ln2_b': (0.0, 0.8)}
    factors = {'L0_xcond_attn1_bo': 8.0,
     'L0_xcond_attn2_bo': 8.0,
     'L0_xcond_ff_b1': 8.0,
     'L0_xcond_ff_b2': 8.0,
     'L0_xcond_norm1_b': 5.523,
     'L0_xcond_norm2_b': 8.0,
     'L0_xcond_norm3_b': 8.0,
     'L0_ffn_router_w': 8.0,
     'L0_ffn_shared_gate_w': 8.0,
     'L0_ffn_shared_up_w': 8.0,
     'L0_ffn_shared_down_w': 8.0,
     'L0_ffn_expert_gate_k': 8.0,
     'L0_ffn_expert_up_k': 8.0,
     'L0_ffn_expert_down_k': 8.0,
     'L1_xcond_Wq': 8.0,
     'L1_ffn_W1': 4.805,
     'L1_ffn_b1': 8.0,
     'L1_ffn_W2': 4.521,
     'L1_ffn_b2': 48.845,
     'L1_ffn_Wr': 4.423,
     'L1_ffn_br': 8.0}
    for name, (base, spread) in spreads.items():
        noise = np.random.default_rng([zlib.crc32(name.encode()), seed]).standard_normal(out[name].shape)
        drawn = base * np.exp(spread * noise) if base else spread * noise
        out[name] = jnp.asarray(drawn.astype(out[name].dtype))
    for name, factor in factors.items():
        out[name] = (out[name] * factor).astype(out[name].dtype)
    return out
```

```python
from contextlib import ExitStack

import concourse.bass as bass
from concourse import mybir

F32 = mybir.dt.float32
I32 = mybir.dt.int32
ALU = mybir.AluOpType
ACT = mybir.ActivationFunctionType
AXX = mybir.AxisListType.X
PE, DVE = mybir.EngineType.PE, mybir.EngineType.DVE

B, T, D = 16, 112, 256
S = 375
H, DH = 16, 64
INNER = H * DH
P = 128
DC = D // P
IC = INNER // P
SC = 125
NS = S // SC
KV = S + T
KC = 122
NK = 4
DFF = 1024
FC = DFF // P
EPS = 1e-5
QSCALE = 1.0 / 8.0
TOK = B * T
RSQRT_SEED = float(0x5F3759DF)


class Tally:

    def __init__(self):
        self.base, self.k, self.off, self.start, self.per = 0, 0, 0, None, 0

    @property
    def turn(self):
        return (self.off + self.k - 1) % 2

    def next(self, n=1):
        self.k += n
        return self.base + self.k

    def now(self):
        return self.base + self.k

    def enter(self, i, per):
        self.off += self.k
        if self.k:
            self.start, self.k = self.base + self.k, 0
        elif self.start is None:
            self.start = self.base
        self.per = per
        self.base = self.start + i * per

    def leave(self, turns):
        assert self.k == self.per, (self.k, self.per)
        self.base, self.k, self.off = self.start + turns * self.per, 0, self.off + self.k
        self.start = None


class Experts:

    def __init__(self, n, experts, topk, ring, wsize):
        self.n, self.E, self.K, self.R, self.wsize = n, experts, topk, ring, wsize
        self.NBLK = -(-(TOK * topk // P + experts) // 4) * 4
        self.NBUF = 4


class At:

    def __init__(self, turn, i):
        self.turn = turn + i // 4
        self.m = i % 4
        self.m2 = i % 2
        self.j = 4 * turn + i


def build(nc, a, out, stop=None):
    with ExitStack() as ctx:
        def sb(name, shape, dt=F32):
            return ctx.enter_context(nc.sbuf_tensor(name, shape, dt))

        def ps(name, shape):
            return ctx.enter_context(nc.psum_tensor(name, shape, F32))

        def sem(name):
            return ctx.enter_context(nc.semaphore(name))

        X = sb("X", [T, B, D])
        W = sb("W", [P, 22528])
        ident = sb("ident", [P, P])
        condT = sb("condT", [P, DC, B])
        cols = sb("cols", [P, 100])
        aff = sb("aff", [P, 12, B])
        rows = sb("rows", [T, 3, D])
        mu1, rs1 = sb("mu1", [T, B]), sb("rs1", [T, B])
        mu2, rs2 = sb("mu2", [T, B]), sb("rs2", [T, B])
        hT1, hT2 = sb("hT1", [P, DC, T]), sb("hT2", [P, DC, T])
        qT1, kT1 = sb("qT1", [P, IC, T]), sb("kT1", [P, IC, T])
        v1 = sb("v1", [P, 1, INNER])
        qT2 = qT1
        kT2 = sb("kT2", [P, IC, KV])
        v2 = sb("v2", [SC, NK, INNER])
        ctxT = sb("ctxT", [P, DC, KV])
        osb = sb("osb", [T, INNER])
        oT = sb("oT", [P, IC, T])
        probs = sb("probs", [T, 4, KV])
        probsT = sb("probsT", [SC, 2, 4 * T])
        nmax, rsum, rinv = sb("nmax", [T, H]), sb("rsum", [T, H]), sb("rinv", [T, H])
        mlp = sb("mlp", [P, 3072])
        gel = mlp[:, 0:FC * T].rearrange("p (f t) -> p f t", f=FC)
        uT = mlp[:, FC * T:2 * FC * T].rearrange("p (f t) -> p f t", f=FC)
        R1, R1b, R2, R2b = (sb(n, [T, D]) for n in ("R1", "R1b", "R2", "R2b"))
        xs, xn, xnb, hn1, hn2 = (sb(n, [T, D]) for n in ("xs", "xn", "xnb", "hn1", "hn2"))
        ctxr, ctxn = (v[0:SC].rearrange("p c n -> p (c n)")[:, 0:NS * D].rearrange("p (c d) -> p c d", c=NS)
                      for v in (kT1, v1))
        latn = R2
        affL = sb("affL", [P, 4, B])
        cst, cmv = sb("cst", [P, 4, 6]), sb("cmv", [P, 4, 2])
        cve, crt, cry = sb("cve", [P, 4]), sb("crt", [P, 4]), sb("cry", [P, 4])
        st, mv = sb("st", [P, B, 6]), sb("mv", [P, B, 2])
        ve, rt, ry = sb("ve", [P, B]), sb("rt", [P, B]), sb("ry", [P, B])

        L0E, L1E = Experts(0, 64, 8, 8, 768), Experts(1, 8, 1, 2, 5376)
        ones = sb("ones", [P, P])
        before = sb("before", [P, P])
        upto = sb("upto", [64, 64])
        iotaf = sb("iotaf", [P, L0E.NBLK])
        iotai = sb("iotai", [P, L0E.NBLK], I32)
        tok = sb("tok", [T, B], I32)
        fill = sb("fill", [P, L0E.NBLK], I32)
        rw0, rw1 = sb("rw0", [P, DC, 64]), sb("rw1", [P, DC, 8])
        br = sb("br", [T, 8])
        hTr = mlp[:, 0:4 * DC * T].rearrange("p (u c t) -> p u c t", u=4, c=DC)
        hall = v2[0:T].rearrange("t c n -> t (c n)").rearrange("t (b d) -> t b d", b=B)
        flat = kT2[:].rearrange("p c n -> p (c n)")
        sc = flat[0:T, 0:1024]
        msk = flat[0:T, 1024:2048]
        cum = flat[0:T, 2048:3136]
        slotv = probs[:].rearrange("t u k -> t (u k)")[:, 0:1024]
        tmpv = probs[:].rearrange("t u k -> t (u k)")[:, 1024:1088]
        rep_ = osb[:]
        top = sb("top", [T, B, 8])
        topi = sb("topi", [T, B, 8], mybir.dt.uint32)
        topf = sb("topf", [T, B, 8])
        wgt = sb("wgt", [T, B, 8])
        slotf = sb("slotf", [T, B, 8])
        sloti, slotj, desti = (sb(n, [T, B, 8], I32) for n in ("sloti", "slotj", "desti"))
        ecol = sb("ecol", [64, 8])
        ecoli = sb("ecoli", [64, 1], I32)
        oflat = oT[:].rearrange("p c t -> p (c t)")
        bmat, gmat, startS = oflat[0:64, 0:P], oflat[0:64, P:2 * P + L0E.NBLK], oflat[0:T, 512:576]
        brow = sb("brow", [1, L0E.NBLK], I32)
        rrow = sb("rrow", [1, 64], I32)
        lrow = sb("lrow", [1, 64], I32)
        ids = sb("ids", [P, L0E.NBLK], I32)
        idc = sb("idc", [P, 4], I32)
        st8 = sb("st8", [T, 2, 8], I32)
        stt = sb("stt", [T, 2], I32)
        xg = flat[:, 0:1024].rearrange("p (u d) -> p u d", u=4)
        xT = flat[:, 1024:1536].rearrange("p (u c t) -> p u c t", u=2, c=DC)
        sg = mlp[:, 1024:1280].rearrange("p (u i) -> p u i", u=2)
        hh = mlp[:, 1280:1536].rearrange("p (u i) -> p u i", u=2)
        hhT = mlp[:, 1536:1792].rearrange("p (u i) -> p u i", u=2)
        ysb = flat[:, 2304:3328].rearrange("p (u d) -> p u d", u=4)
        shw = W[:, 14336:15104]
        h1b, h1g, h1T = (mlp[:, 1024 * i:1024 * (i + 1)] for i in range(3))
        yk = mlp[0:T, 0:2048].rearrange("t (k d) -> t k d", k=8)
        RING = 8192

        psG = ps("psG", [P, 4, 512])
        psT = ps("psT", [P, 2, 512])
        psO = ps("psO", [P, 2, 512])

        def wview(off, c, n):
            return W[:, off:off + c * n].rearrange("p (c n) -> p c n", c=c)

        wq1, wk1, wv1, wq2, wk2, wv2 = (wview(2048 * i, 2, 1024) for i in range(6))
        wo1, wo2 = wview(12288, 8, 256), wview(14336, 8, 256)
        fw1, fw2 = wview(16384, 2, 2048), wview(20480, 8, 256)

        wqL, wkvL, woL = wview(0, 2, 1024), wview(2048, 2, 2048), wview(6144, 8, 256)

        NB, FB = 0, 12
        LN1W, LN1B, LN2W, LN2B = 28, 30, 32, 34
        MB1 = 36

        small_in = sem("small_in")
        x_in = sem("x_in")
        w_in = {n: sem("w_in_" + n) for n in ("nw", "q1", "k1", "v1", "o1", "k2", "v2", "q2", "o2", "f1", "f2")}
        ctx_in = sem("ctx_in")
        consts = sem("consts")
        stats_done = sem("stats_done")
        aff_done = sem("aff_done")
        act_full, act_evac = sem("act_full"), sem("act_evac")
        dve_full, dve_evac = sem("dve_full"), sem("dve_evac")
        scores_ready, max_ready, probs_ready = sem("scores_ready"), sem("max_ready"), sem("probs_ready")
        probsT_ready = sem("probsT_ready")
        copied_act, copied_dve = sem("copied_act"), sem("copied_dve")
        outputs_ready, osb_ready = sem("outputs_ready"), sem("osb_ready")
        dve_step, pool_step = sem("dve_step"), sem("pool_step")
        r1b_ready, r2b_ready = sem("r1b_ready"), sem("r2b_ready")
        hn1_ready, hn2_ready = sem("hn1_ready"), sem("hn2_ready")
        out_done = sem("out_done")
        wL_in, ctxr_in = sem("wL_in"), sem("ctxr_in")
        lat_stats, lat_ready = sem("lat_stats"), sem("lat_ready")
        x3_done = sem("x3_done")
        sh_in = sem("sh_in")

        def wait_apart(eng, s, value):
            value = value if isinstance(value, int) else eng.snap(eng.to_reg(value))
            eng.wait_ge(consts, 1)
            eng.wait_ge(s, value)

        def inverse_root(engine, chain, y, var, t, v):
            chain(engine.tensor_scalar(v, var, EPS, None, ALU.add))
            chain(engine.tensor_scalar(y.bitcast(I32), v.bitcast(I32), -0.5, RSQRT_SEED, ALU.mult, ALU.add))
            for _ in range(3):
                chain(engine.tensor_tensor(t, y, y, ALU.mult))
                chain(engine.tensor_tensor(t, t, v, ALU.mult))
                chain(engine.tensor_scalar(t, t, -0.5, 1.5, ALU.mult, ALU.add))
                chain(engine.tensor_tensor(y, y, t, ALU.mult))

        def ranks_of(engine, l, first, n):
            return nc.values_load_multi_w_load_instructions(brow[0:1, bass.ds(first, n)], engines=[engine], min_val=0,
                                                            max_val=l.E - 1)[1]

        class Signals:

            def __init__(self, n, ring):
                self.normed = sem(f"normed{n}")
                self.h_stored = sem(f"h_stored{n}")
                self.hT_ready = sem(f"hT_ready{n}")
                self.logits_full = sem(f"logits_full{n}")
                self.scores_ok = sem(f"scores_ok{n}")
                self.mask_ok = sem(f"mask_ok{n}")
                self.counts_full = sem(f"counts_full{n}")
                self.blocks_ok = sem(f"blocks_ok{n}")
                self.incl_full = sem(f"incl_full{n}")
                self.incl_ok = sem(f"incl_ok{n}")
                self.rows_full = sem(f"rows_full{n}")
                self.tables = sem(f"tables{n}")
                self.ranks_full = sem(f"ranks_full{n}")
                self.slots_ok = sem(f"slots_ok{n}")
                self.staged = sem(f"staged{n}")
                self.scat_a = sem(f"scat_a{n}")
                self.scat_b = sem(f"scat_b{n}")
                self.ids_in = sem(f"ids_in{n}")
                self.loaded = sem(f"loaded{n}")
                self.xT_full = sem(f"xT_full{n}")
                self.xT_done = sem(f"xT_done{n}")
                self.gu_full = sem(f"gu_full{n}")
                self.sg_done = sem(f"sg_done{n}")
                self.h_done = sem(f"h_done{n}")
                self.hT_full = sem(f"hT_full{n}")
                self.hT_done = sem(f"hT_done{n}")
                self.y_full = sem(f"y_full{n}")
                self.y_done = sem(f"y_done{n}")
                self.combined = sem(f"combined{n}")
                self.route_a = sem(f"route_a{n}")
                self.table_filled = sem(f"table_filled{n}")
                if n == 0:
                    self.sh_gu = sem("sh_gu")
                    self.sh_sg = sem("sh_sg")
                    self.sh_h = sem("sh_h")
                    self.sh_hT = sem("sh_hT")
                    self.sh_hTc = sem("sh_hTc")
                    self.sh_y = sem("sh_y")
                    self.sh_done = sem("sh_done")
                else:
                    self.exps = sem("exps")
                    self.hT_done2 = sem("hT_done2")
                self.xg_in = [sem(f"xg_in{n}_{i}") for i in range(4)]
                self.ring_in = [sem(f"ring_in{n}_{i}") for i in range(ring)]
                self.y_stored = [sem(f"y_stored{n}_{i}") for i in range(4)]
                self.yk_in = [sem(f"yk_in{n}_{i}") for i in range(2)]

        def units1():
            return [[h0 + 2 * i for i in range(4)] for h0 in (0, 1, 8, 9)]

        def units2():
            return [[h] for h in range(H)]

        ACT_JOBS, DVE_JOBS, R1_JOB, R2_JOB = 18, 18, 6, 14
        BLOCK1_JOBS = 4 + B * DVE_JOBS - 3
        ACTL_JOBS, DVEL_JOBS = 11, 12
        BANK = (0, 2, 1, 3)

        def chunks(keys, size):
            return [(k, min(size, keys - k)) for k in range(0, keys, size)]

        def half_end(units):
            n = len(units)
            return (n // 2 - 1, n - 1)

        def on_act(u):
            return u % 4 == 3

        S0, S1 = Signals(0, L0E.R), Signals(1, L1E.R)
        hd = nc.dram_tensor("normed_rows", (TOK, D), F32, kind="Internal").ap()
        table = {l.n: nc.dram_tensor(f"slot_table{l.n}", (P * l.NBLK, 1), I32, kind="Internal").ap() for l in (L0E, L1E)}
        ydram = {l.n: nc.dram_tensor(f"expert_rows{l.n}", (P * l.NBLK, D), F32, kind="Internal").ap() for l in (L0E, L1E)}
        LAYERS = ((L0E, S0), (L1E, S1))

        block = ctx.enter_context(nc.Block())

        @block.sync
        def _(sp):
            sp.dma_start(X[:], a["x"].rearrange("b t d -> t b d")).then_inc(x_in, 16)
            sp.dma_start(condT[:], a["condT"].rearrange("(c p) b -> p c b", p=P)).then_inc(small_in, 16)
            sp.dma_start(cols[:], a["cols"]).then_inc(small_in, 16)
            sp.dma_start(rows[:], a["rows"].partition_broadcast(T)).then_inc(small_in, 16)
            nw = wview(16384, 6, 512)
            sp.dma_start(nw, a["nw"].rearrange("n (c p) m -> p (n c) m", p=P)).then_inc(w_in["nw"], 16)

            def load(view, name, src):
                sp.dma_start(view, a[src].rearrange("(c p) n -> p c n", p=P)).then_inc(w_in[name], 16)

            sp.dma_start(rw0[:], a["rw0"].rearrange("(c p) e -> p c e", p=P)).then_inc(small_in, 16)
            sp.dma_start(rw1[:], a["rw1"].rearrange("(c p) e -> p c e", p=P)).then_inc(small_in, 16)
            sp.dma_start(br[:], a["br"].partition_broadcast(T)).then_inc(small_in, 16)
            sp.wait_ge(consts, 8)
            for l, s in LAYERS:
                sp.dma_start(table[l.n].rearrange("(p j) o -> p (j o)", p=P), fill[:, 0:l.NBLK]).then_inc(s.table_filled, 16)
            load(wq1, "q1", "wq1")
            load(wk1, "k1", "wk1")
            load(wv1, "v1", "wv1")
            sp.dma_start(ctxT[:, :, 0:S], a["ctxT"][0].rearrange("(c p) s -> p c s", p=P)).then_inc(ctx_in, 16)
            load(wk2, "k2", "wk2")
            load(wo1, "o1", "wo1")
            load(wv2, "v2", "wv2")
            load(wq2, "q2", "wq2")
            load(wo2, "o2", "wo2")
            sp.wait_ge(aff_done, 1)
            load(fw1, "f1", "fw1")
            load(fw2, "f2", "fw2")
            with sp.Fori(0, B - 1) as b:
                sp.wait_ge(hn2_ready, 2 * b + 2)
                sp.dma_start(ctxT[:, :, 0:S],
                             a["ctxT"][bass.ds(b + 1, 1)].rearrange("o (c p) s -> p (o c) s", p=P)).then_inc(ctx_in, 16)
            sp.wait_ge(dve_evac, BLOCK1_JOBS)
            sp.dma_start(shw, a["shw"]).then_inc(sh_in, 16)

            def experts(l, s):
                sp.wait_ge(s.normed, B)
                sp.dma_start(hd.rearrange("(b t) d -> t b d", t=T), hall).then_inc(s.h_stored, 16)
                sp.wait_ge(s.scat_a, 16 * l.K * B // 2)
                sp.wait_ge(s.scat_b, 16 * l.K * B // 2)
                sp.dma_start(ids[:, 0:l.NBLK], table[l.n].rearrange("(p j) o -> p (j o)", p=P)).then_inc(s.ids_in, 16)
                sp.wait_ge(s.tables, 1)

                def weights(turn, i, wait):
                    rank = l.R * turn + i
                    if wait:
                        last = sp.value_load(lrow[0:1, bass.ds(rank - l.R, 1)], min_val=0, max_val=l.NBLK)
                        if l.n == 0:
                            sp.wait_ge(s.y_full, last + 1)
                        else:
                            sp.wait_ge(s.y_done, last)
                    e = sp.value_load(rrow[0:1, bass.ds(rank, 1)], min_val=0, max_val=l.E - 1)
                    dst = W[:, RING + i * l.wsize:RING + (i + 1) * l.wsize]
                    if l.n == 0:
                        sp.dma_start(dst, a["ew0"][bass.ds(e, 1)].rearrange("o p n -> (o p) n")).then_inc(s.ring_in[i], 16)
                    else:
                        sp.dma_start(dst[:, 0:4096], a["ew1"][bass.ds(e, 1)].rearrange("o p n -> (o p) n")).then_inc(s.ring_in[i], 16)
                        sp.dma_start(dst[:, 4096:5376], a["eb1"][bass.ds(e, 1)].rearrange("o n -> (o n)").partition_broadcast(P)).then_inc(s.ring_in[i], 16)

                def arrived(turn, i):
                    sp.wait_ge(s.ring_in[i], (16 if l.n == 0 else 32) * (turn + 1))
                    sp.sem_inc(s.loaded, 1)

                for i in range(l.R):
                    weights(0, i, False)
                for i in range(l.R):
                    arrived(0, i)
                with sp.Fori(1, l.E // l.R) as turn:
                    late = l.R > 4
                    for i in range(l.R):
                        weights(turn, i, True)
                        if i or not late:
                            arrived(turn, i - late)
                    if late:
                        arrived(turn, l.R - 1)

            sp.dma_start(wqL, a["wqL"].rearrange("(c p) n -> p c n", p=P)).then_inc(wL_in, 16)
            sp.dma_start(wkvL, a["wkvL"].rearrange("(c p) n -> p c n", p=P)).then_inc(wL_in, 16)
            sp.dma_start(woL, a["woL"].rearrange("(c p) n -> p c n", p=P)).then_inc(wL_in, 16)
            sp.dma_start(ctxr[:], a["ctx"][0].rearrange("(c p) d -> p c d", p=SC)).then_inc(ctxr_in, 16)
            experts(L0E, S0)
            with sp.Fori(1, B) as b:
                sp.wait_ge(lat_ready, b)
                sp.dma_start(ctxr[:], a["ctx"][bass.ds(b, 1)].rearrange("o (c p) d -> p (o c) d", p=SC)).then_inc(ctxr_in, 16)
            sp.wait_ge(x3_done, B)
            experts(L1E, S1)
            sp.wait_ge(S1.combined, B)
            sp.dma_start(out.rearrange("b t d -> t b d"), X[:]).then_inc(out_done, 16)
            sp.wait_ge(out_done, 16)

        @block.gpsimd
        def _(pool):
            nc.gpsimd.memset(ident[:], 0.0).then_inc(consts, 1)
            pool.wait_ge(consts, 1)
            nc.gpsimd.affine_select(out=ident[:], in_=ident[:], compare_op=ALU.not_equal, fill=1.0, base=0,
                                    pattern=[[-1, P]], channel_multiplier=1).then_inc(consts, 1)
            nc.gpsimd.memset(ones[:], 1.0).then_inc(consts, 1)
            nc.gpsimd.memset(upto[:], 1.0).then_inc(consts, 1)
            nc.gpsimd.memset(fill[:], 0).then_inc(consts, 1)
            pool.wait_ge(consts, 5)
            nc.gpsimd.affine_select(out=before[:], in_=ones[:], compare_op=ALU.is_ge, fill=0.0, base=-1,
                                    pattern=[[1, P]], channel_multiplier=-1).then_inc(consts, 1)
            nc.gpsimd.affine_select(out=upto[:], in_=upto[:], compare_op=ALU.is_ge, fill=0.0, base=0,
                                    pattern=[[1, 64]], channel_multiplier=-1).then_inc(consts, 1)
            nc.gpsimd.iota(iotai[:], [[1, L0E.NBLK]], base=0, channel_multiplier=0)
            nc.gpsimd.iota(tok[:], [[T, B]], base=0, channel_multiplier=1).then_inc(consts, 1)
            step = Tally()

            def chain(ins):
                ins.then_inc(pool_step, 1)
                wait_apart(pool, pool_step, step.next())

            def norm1(b):
                one = bass.ds(b, 1)
                xb = X[:, one, :].rearrange("t o d -> t (o d)")
                chain(nc.gpsimd.tensor_tensor(xs[:], xb, mu1[:, one].broadcast_to([T, D]), ALU.subtract))
                chain(nc.gpsimd.tensor_tensor(xn[:], xs[:], rs1[:, one].broadcast_to([T, D]), ALU.mult))
                chain(nc.gpsimd.tensor_tensor(xs[:], xn[:], mu2[:, one].broadcast_to([T, D]), ALU.subtract))
                chain(nc.gpsimd.tensor_tensor(hn1[:], xs[:], rs2[:, one].broadcast_to([T, D]), ALU.mult))
                nc.gpsimd.tensor_tensor(xnb[:], xn[:], rows[:, 0, :], ALU.add).then_inc(hn1_ready, 1)

            pool.wait_ge(small_in, 96)
            pool.wait_ge(x_in, 16)
            pool.wait_ge(stats_done, 1)
            norm1(0)

            def batch(b, last):
                pool.wait_ge(dve_evac, 4 + DVE_JOBS * b + R1_JOB)
                nc.gpsimd.tensor_tensor(R1b[:], R1[:], rows[:, 1, :], ALU.add).then_inc(r1b_ready, 1)
                if not last:
                    norm1(b + 1)
                wait_apart(pool, dve_evac, 4 + DVE_JOBS * b + R2_JOB - 2 * last)
                chain(nc.gpsimd.tensor_tensor(R2b[:], R2[:], rows[:, 2, :], ALU.add))
                nc.gpsimd.tensor_tensor(R2b[:], R2b[:], X[:, bass.ds(b, 1), :].rearrange("t o d -> t (o d)"),
                                        ALU.add).then_inc(r2b_ready, 1)

            with pool.Fori(0, B - 1) as b:
                step.enter(b, 5)
                batch(b, False)
            step.leave(B - 1)
            batch(B - 1, True)

            def experts(l, s):
                pool.wait_ge(s.slots_ok, 1)
                pool.wait_ge(s.table_filled, 16)
                pool.wait_ge(s.h_stored, 16)
                done = (s.scat_a, s.scat_b)

                def scatter(turn, u, reuse):
                    if reuse:
                        wait_apart(pool, done[u], 16 * l.K * turn)
                    tile = 2 * turn + u
                    nc.gpsimd.tensor_copy(st8[:, u, :], desti[:, bass.ds(tile, 1), :].rearrange("t o k -> t (o k)"))
                    nc.gpsimd.tensor_copy(stt[:, u:u + 1], tok[:, bass.ds(tile, 1)]).then_inc(s.staged, 1)
                    wait_apart(pool, s.staged, tile + 1)
                    for k in range(l.K):
                        nc.gpsimd.indirect_dma_start(
                            out=table[l.n], out_offset=bass.IndirectOffsetOnAxis(ap=st8[:, u, k:k + 1], axis=0),
                            in_=stt[:, u:u + 1], in_offset=None).then_inc(done[u], 16)

                scatter(0, 0, False)
                scatter(0, 1, False)
                with pool.Fori(1, B // 2) as turn:
                    scatter(turn, 0, True)
                    scatter(turn, 1, True)

                pool.wait_ge(s.ids_in, 16)

                def gather(j, reuse):
                    if reuse:
                        wait_apart(pool, s.xT_full, j.j - 3)
                    nc.gpsimd.tensor_copy(idc[:, j.m:j.m + 1], ids[:, bass.ds(j.j, 1)]).then_inc(s.staged, 1)
                    wait_apart(pool, s.staged, B + j.j + 1)
                    nc.gpsimd.indirect_dma_start(
                        out=xg[:, j.m, :], out_offset=None, in_=hd,
                        in_offset=bass.IndirectOffsetOnAxis(ap=idc[:, j.m:j.m + 1], axis=0)).then_inc(s.xg_in[j.m], 16)

                for i in range(4):
                    gather(At(0, i), False)
                with pool.Fori(1, l.NBLK // 4) as turn:
                    for i in range(4):
                        gather(At(turn, i), True)

                for i in range(4):
                    pool.wait_ge(s.y_stored[i], 16 * (l.NBLK // 4) + 16)

            def fetch0(b, reuse):
                if reuse:
                    wait_apart(pool, S0.combined, b)
                nc.gpsimd.tensor_copy(st8[:, 0, :], sloti[:, bass.ds(b, 1), :].rearrange("t o k -> t (o k)")).then_inc(S0.staged, 1)
                wait_apart(pool, S0.staged, B + L0E.NBLK + b + 1)
                for k in range(L0E.K):
                    nc.gpsimd.indirect_dma_start(
                        out=yk[:, k, :], out_offset=None, in_=ydram[0],
                        in_offset=bass.IndirectOffsetOnAxis(ap=st8[:, 0, k:k + 1], axis=0)).then_inc(S0.yk_in[0], 16)

            def fetch1(l, s):

                def fetch(turn, u, reuse):
                    tile = 2 * turn + u
                    if reuse:
                        wait_apart(pool, s.combined, tile - 1)
                    nc.gpsimd.tensor_copy(st8[:, u, :], sloti[:, bass.ds(tile, 1), :].rearrange("t o k -> t (o k)")).then_inc(s.staged, 1)
                    wait_apart(pool, s.staged, B + l.NBLK + tile + 1)
                    for k in range(l.K):
                        nc.gpsimd.indirect_dma_start(
                            out=yk[:, u, :], out_offset=None, in_=ydram[l.n],
                            in_offset=bass.IndirectOffsetOnAxis(ap=st8[:, u, k:k + 1], axis=0)).then_inc(s.yk_in[u], 16)

                fetch(0, 0, False)
                fetch(0, 1, False)
                with pool.Fori(1, B // 2) as turn:
                    fetch(turn, 0, True)
                    fetch(turn, 1, True)

            experts(L0E, S0)

            def normalise_rows(b):
                wait_apart(pool, lat_stats, b + 1)
                inverse_root(nc.gpsimd, chain, cry[:], cmv[:, :, 1], crt[:], cve[:])
                chain(nc.gpsimd.tensor_tensor(ry[:, 0:1], cmv[:, 3, 1:2], cry[:, 3:4], ALU.mult))
                chain(nc.gpsimd.tensor_tensor(ry[:, 0:1], ry[:, 0:1], cry[:, 3:4], ALU.mult))
                inverse_root(nc.gpsimd, chain, ry[:, 1:2], ry[:, 0:1], rt[:, 0:1], ve[:, 0:1])
                for c in range(NS):
                    nc.gpsimd.tensor_scalar(ctxn[:, c, :], ctxr[:, c, :], cmv[0:SC, c, 0:1], cry[0:SC, c:c + 1],
                                            ALU.subtract, ALU.mult)
                chain(nc.gpsimd.tensor_tensor(ry[:, 2:3], ry[:, 1:2], cry[:, 3:4], ALU.mult))
                xb = X[:, bass.ds(b, 1), :].rearrange("t o d -> t (o d)")
                chain(nc.gpsimd.tensor_tensor(latn[:], xb, cmv[0:T, 3, 0:1].broadcast_to([T, D]), ALU.subtract))
                nc.gpsimd.tensor_tensor(latn[:], latn[:], ry[0:T, 2:3].broadcast_to([T, D]), ALU.mult).then_inc(lat_ready, 1)

            fetch0(0, False)
            with pool.Fori(0, B - 1) as b:
                step.enter(b, 32)
                normalise_rows(b)
                fetch0(b + 1, True)
            step.leave(B - 1)
            normalise_rows(B - 1)
            experts(L1E, S1)
            fetch1(L1E, S1)

        @block.tensor
        def _(pe):
            act, dve = Tally(), Tally()
            unit, oc, osbs = Tally(), Tally(), Tally()
            ca, cd = Tally(), Tally()

            def bank_for_act():
                n = act.next()
                if not (isinstance(n, int) and n <= 2):
                    pe.wait_ge(act_evac, n - 2)
                return psG[:, act.turn, :]

            def bank_for_dve():
                n = dve.next()
                if not (isinstance(n, int) and n <= 2):
                    pe.wait_ge(dve_evac, n - 2)
                return psG[:, 2 + dve.turn, :]

            def evacuated():
                pe.wait_ge(act_evac, act.now())
                pe.wait_ge(dve_evac, dve.now())

            def attention(units, qT, kT, v, keys, size):
                n = len(units)
                ch = chunks(keys, size)
                blocks = lambda u: [(h, 0, 0, keys) for h in units[u]] if len(units[u]) > 1 else \
                    [(units[u][0], c, k0, kn) for c, (k0, kn) in enumerate(ch)]
                u0, a0, d0 = unit.now(), ca.now(), cd.now()
                na = nd = 0
                copied = {}
                for u in range(n):
                    if on_act(u):
                        na += 1
                        copied[u] = (copied_act, a0 + na)
                    else:
                        nd += 1
                        copied[u] = (copied_dve, d0 + nd)
                for s in range(n + 3):
                    if s < n:
                        for i, h in enumerate(units[s]):
                            r = DH * (h % 2)
                            mm = nc.tensor.matmul(psG[0:T, BANK[s % 4], i * keys:(i + 1) * keys],
                                                  qT[r:r + DH, h // 2, :], kT[r:r + DH, h // 2, 0:keys],
                                                  start=True, stop=True)
                        mm.then_inc(scores_ready, 1)
                    u = s - 2
                    if 0 <= u < n:
                        pe.wait_ge(probs_ready, u0 + u + 1)
                        for i, (h, c, k0, kn) in enumerate(blocks(u)):
                            off = i * keys if len(units[u]) > 1 else k0
                            mm = nc.tensor.transpose(psT[0:kn, u % 2, i * T:(i + 1) * T],
                                                     probs[:, u % 4, off:off + kn], ident[0:T, 0:T])
                        mm.then_inc(probsT_ready, 1)
                    u = s - 3
                    if 0 <= u < n:
                        pe.wait_ge(*copied[u])
                        bl = blocks(u)
                        for i, (h, c, k0, kn) in enumerate(bl):
                            mm = nc.tensor.matmul(psO[0:T, h // 8, (h % 8) * DH:(h % 8 + 1) * DH],
                                                  probsT[0:kn, u % 2, i * T:(i + 1) * T],
                                                  v[0:kn, c, h * DH:(h + 1) * DH],
                                                  start=(len(units[u]) > 1 or i == 0),
                                                  stop=(len(units[u]) > 1 or i == len(bl) - 1))
                        if u in half_end(units):
                            mm.then_inc(outputs_ready, 1)
                            oc.next()
                unit.next(n)
                ca.next(na)
                cd.next(nd)

            def project_T(wt, hT, n0, nchunks, bank):
                for j in range(nchunks):
                    for c in range(DC):
                        mm = nc.tensor.matmul(bank[:, j * T:(j + 1) * T], wt[:, c, n0 + j * P:n0 + (j + 1) * P],
                                              hT[:, c, :], start=(c == 0), stop=(c == DC - 1))
                return mm

            def keys_T(wt, n0, j, src, n, bank):
                for c in range(DC):
                    mm = nc.tensor.matmul(bank[:, 0:n], wt[:, c, n0 + j * P:n0 + (j + 1) * P], src[:, c, 0:n],
                                          start=(c == 0), stop=(c == DC - 1))
                return mm

            def values(wt, n0, src, k0, kn, half, bank):
                for c in range(DC):
                    mm = nc.tensor.matmul(bank[0:kn, 0:512], src[:, c, k0:k0 + kn],
                                          wt[:, c, n0 + half * 512:n0 + (half + 1) * 512],
                                          start=(c == 0), stop=(c == DC - 1))
                return mm

            def transpose_out():
                for half in range(2):
                    pe.wait_ge(osb_ready, osbs.next())
                    bank = bank_for_act() if half == 0 else bank_for_dve()
                    for j in range(4):
                        mm = nc.tensor.transpose(bank[:, j * T:(j + 1) * T],
                                                 osb[:, (4 * half + j) * P:(4 * half + j + 1) * P], ident[0:T, 0:T])
                    mm.then_inc(act_full if half == 0 else dve_full, 1)

            def project_out(wo, oT_, n):
                bank = bank_for_dve()
                for c in range(n):
                    mm = nc.tensor.matmul(bank[0:T, 0:D], oT_[:, c, :], wo[:, c, :], start=(c == 0), stop=(c == n - 1))
                mm.then_inc(dve_full, 1)

            def transpose_h(hn):
                bank = bank_for_act()
                for c in range(DC):
                    mm = nc.tensor.transpose(bank[:, c * T:(c + 1) * T], hn[:, c * P:(c + 1) * P], ident[0:T, 0:T])
                mm.then_inc(act_full, 1)

            def qk1():
                transpose_h(hn1)
                pe.wait_ge(act_evac, act.now())
                for w, name in ((wq1, "q1"), (wk1, "k1")):
                    if first:
                        pe.wait_ge(w_in[name], 16)
                    project_T(w, hT1, 0, 4, bank_for_act()).then_inc(act_full, 1)
                    project_T(w, hT1, 512, 4, bank_for_dve()).then_inc(dve_full, 1)

            def val1():
                if first:
                    pe.wait_ge(w_in["v1"], 16)
                values(wv1, 0, hT1, 0, T, 0, bank_for_act()).then_inc(act_full, 1)
                values(wv1, 0, hT1, 0, T, 1, bank_for_dve()).then_inc(dve_full, 1)

            pe.wait_ge(consts, 2)
            pe.wait_ge(small_in, 96)
            pe.wait_ge(w_in["nw"], 16)
            nw = wview(16384, 6, 512)
            bank = bank_for_dve()
            for n in range(3):
                for j in range(4):
                    for c in range(DC):
                        mm = nc.tensor.matmul(bank[:, (4 * n + j) * B:(4 * n + j + 1) * B],
                                              nw[:, 2 * n + c, j * P:(j + 1) * P], condT[:, c, :],
                                              start=(c == 0), stop=(c == DC - 1))
            mm.then_inc(dve_full, 1)
            first = True
            pe.wait_ge(hn1_ready, 1)
            qk1()
            val1()
            first = False

            def batch(b, last):
                evacuated()
                attention(units1(), qT1, kT1, v1, T, T)
                pe.wait_ge(ctx_in, 16 * b + 16)
                pe.wait_ge(w_in["k2"], 16)
                for j in range(IC):
                    if j % 2 == 0:
                        keys_T(wk2, 0, j, ctxT, S, bank_for_act()).then_inc(act_full, 1)
                    else:
                        keys_T(wk2, 0, j, ctxT, S, bank_for_dve()).then_inc(dve_full, 1)
                transpose_out()
                evacuated()
                pe.wait_ge(w_in["o1"], 16)
                project_out(wo1, oT, IC)
                pe.wait_ge(w_in["v2"], 16)
                for c in range(NS):
                    values(wv2, 0, ctxT, c * SC, SC, 0, bank_for_act()).then_inc(act_full, 1)
                    values(wv2, 0, ctxT, c * SC, SC, 1, bank_for_dve()).then_inc(dve_full, 1)
                pe.wait_ge(hn2_ready, 2 * b + 1)
                transpose_h(hn2)
                pe.wait_ge(w_in["q2"], 16)
                pe.wait_ge(act_evac, act.now())
                project_T(wq2, hT2, 0, 4, bank_for_act()).then_inc(act_full, 1)
                project_T(wq2, hT2, 512, 4, bank_for_dve()).then_inc(dve_full, 1)
                evacuated()
                attention(units2(), qT2, kT2, v2, S, SC)
                if not last:
                    pe.wait_ge(hn1_ready, b + 2)
                    qk1()
                transpose_out()
                evacuated()
                pe.wait_ge(w_in["o2"], 16)
                project_out(wo2, oT, IC)
                if not last:
                    val1()
                pe.wait_ge(hn2_ready, 2 * b + 2)
                transpose_h(hn2)
                pe.wait_ge(act_evac, act.now())
                pe.wait_ge(w_in["f1"], 16)
                for half in range(2):
                    project_T(fw1, hT2, DFF + 512 * half, 4, bank_for_act()).then_inc(act_full, 1)
                    project_T(fw1, hT2, 512 * half, 4, bank_for_dve()).then_inc(dve_full, 1)
                pe.wait_ge(w_in["f2"], 16)
                pe.wait_ge(dve_evac, dve.now())
                project_out(fw2, uT, FC)

            with pe.Fori(0, B - 1) as b:
                act.enter(b, ACT_JOBS)
                dve.enter(b, DVE_JOBS)
                unit.enter(b, 20)
                ca.enter(b, 5)
                cd.enter(b, 15)
                oc.enter(b, 4)
                osbs.enter(b, 4)
                batch(b, False)
            for t in (act, dve, unit, ca, cd, oc, osbs):
                t.leave(B - 1)
            batch(B - 1, True)

            def route(l, s):
                rw = rw0 if l.n == 0 else rw1
                pe.wait_ge(consts, 8)
                if l.n == 0:
                    pe.wait_ge(sh_in, 16)
                for b in range(B + 3):
                    if b < B:
                        pe.wait_ge(s.normed, b + 1)
                        if b:
                            pe.wait_ge(s.hT_ready, b)
                        for c in range(DC):
                            mm = nc.tensor.transpose(psG[:, 0, c * T:(c + 1) * T], hall[:, b, c * P:(c + 1) * P],
                                                     ident[0:T, 0:T])
                        mm.then_inc(s.route_a, 1)
                    if 0 <= b - 1 < B:
                        logits(l, s, rw, b - 1)
                        if l.n == 0:
                            for c in range(DC):
                                mm = nc.tensor.matmul(psG[0:T, 1 + (b - 1) % 2, 0:256], hTr[:, (b - 1) % 4, c, :],
                                                      shw[:, 256 * c:256 * (c + 1)], start=(c == 0), stop=(c == DC - 1))
                            mm.then_inc(s.sh_gu, 1)
                    if l.n == 0 and 0 <= b - 3:
                        pe.wait_ge(s.sh_hTc, b - 2)
                        if b >= 5:
                            pe.wait_ge(s.sh_done, b - 4)
                        nc.tensor.matmul(psT[0:T, (b - 3) % 2, 0:D], hhT[:, (b - 3) % 2, 0:T], shw[:, 512:768],
                                         start=True, stop=True).then_inc(s.sh_y, 1)
                    if l.n == 0 and 0 <= b - 2 < B:
                        pe.wait_ge(s.sh_h, b - 1)
                        nc.tensor.transpose(psG[:, 3, 0:T], hh[0:T, b % 2, :], ident[0:T, 0:T]).then_inc(s.sh_hT, 1)
                pe.wait_ge(s.mask_ok, 1)
                E = l.E
                nc.tensor.matmul(psG[0:E, 0, 0:1], cum[:, B * E:(B + 1) * E], ones[0:T, 0:1], start=True,
                                 stop=True).then_inc(s.counts_full, 1)
                half = B // 2 * E if l.n == 0 else B * E
                for i in range(B * E // half):
                    nc.tensor.matmul(psO[0:T, i, 0:half], ones[0:T, 0:T], cum[:, i * half:(i + 1) * half],
                                     start=True, stop=False)
                    mm = nc.tensor.matmul(psO[0:T, i, 0:half], before[0:T, 0:T], msk[:, i * half:(i + 1) * half],
                                          start=False, stop=True)
                mm.then_inc(s.ranks_full, 1)
                pe.wait_ge(s.blocks_ok, 1)
                nc.tensor.matmul(psG[:, 1, 0:E], bmat[0:E, :], before[0:E, 0:E], start=True, stop=True)
                nc.tensor.matmul(psG[0:E, 1, 64:66], upto[0:E, 0:E], ecol[0:E, 1:3], start=True,
                                 stop=True).then_inc(s.incl_full, 1)
                pe.wait_ge(s.incl_ok, 1)
                NB_ = l.NBLK
                nc.tensor.matmul(psG[0:1, 2, 0:NB_], ecol[0:E, 2:3], gmat[0:E, 0:NB_], start=True, stop=True)
                nc.tensor.matmul(psG[0:1, 2, 256:256 + E], ones[0:E, 0:1], gmat[0:E, NB_:NB_ + E], start=True, stop=True)
                nc.tensor.matmul(psG[0:1, 2, 320:320 + E], ecol[0:E, 1:2], gmat[0:E, NB_ + E:NB_ + 2 * E], start=True,
                                 stop=True).then_inc(s.rows_full, 1)

            def logits(l, s, rw, b):
                pe.wait_ge(s.hT_ready, b + 1)
                per = 8 if l.n == 0 else 16
                for c in range(DC):
                    mm = nc.tensor.matmul(psO[0:T, b // per, (b % per) * l.E:(b % per + 1) * l.E],
                                          hTr[:, b % 4, c, :], rw[:, c, :], start=(c == 0), stop=(c == DC - 1))
                if b % per == per - 1:
                    mm.then_inc(s.logits_full, 1)

            def blocks(l, s):
                pe.wait_ge(s.tables, 1)
                pe.sem_inc(s.y_full, 1)

                def step(turn, i, lo, hi, ranks):
                    j = At(turn, i)
                    if hi:
                        pe.wait_ge(s.xg_in[j.m], 16 * (j.turn + 1))
                        if l.n == 1 and lo >= 1:
                            pe.wait_ge(s.xT_done, j.j)
                        for c in range(DC):
                            mm = nc.tensor.transpose(pT(l, j)[:, c * P:(c + 1) * P], xg[:, j.m, c * P:(c + 1) * P],
                                                     ident[:])
                        mm.then_inc(s.xT_full, 1)
                    j = At(turn, i - 2)
                    if lo >= 2:
                        pe.wait_ge(s.h_done, j.j + 1)
                        turn_h(l, s, j)
                    j = At(turn, i - 1)
                    if lo >= 1 and (hi or i < 1):
                        rank = ranks[i + 1]
                        pe.wait_ge(s.xT_done, j.j + 1)
                        pe.wait_ge(s.loaded, rank + 1)
                        if l.n == 1 and lo >= 2:
                            pe.wait_ge(s.sg_done, 2 * j.j)
                        up(l, s, j, rank)
                    j = At(turn, i - 2)
                    if lo >= 2:
                        pe.wait_ge(s.hT_done, j.j + 1)
                        if l.n == 1:
                            pe.wait_ge(s.hT_done2, j.j + 1)
                        if not (isinstance(j.j, int) and j.j < 2):
                            pe.wait_ge(s.y_done, j.j - 1)
                        down(l, s, j, ranks[i])

                ranks = (0, 0) + tuple(ranks_of(PE, l, 0, 4))
                for i in range(4):
                    step(0, i, i, True, ranks)
                with pe.Fori(1, l.NBLK // 4) as turn:
                    ranks = ranks_of(PE, l, 4 * turn - 2, 6)
                    for i in range(4):
                        step(turn, i, 4, True, ranks)
                ranks = ranks_of(PE, l, l.NBLK - 2, 2)
                for i in range(2):
                    step(l.NBLK // 4, i, 4, False, ranks)

            def pT(l, j):
                return psG[:, j.m2, :] if l.n == 0 else psT[:, 0, :]

            def ring_at(l, rank):
                return RING + (rank % l.R) * l.wsize

            def up(l, s, j, rank):
                base = ring_at(l, rank)
                if l.n == 0:
                    for c in range(DC):
                        mm = nc.tensor.matmul(psG[:, 2 + j.m2, 0:256], xT[:, j.m2, c, :],
                                              W[:, bass.ds(base + 256 * c, 256)], start=(c == 0), stop=(c == DC - 1))
                    mm.then_inc(s.gu_full, 1)
                else:
                    for h in range(2):
                        for c in range(DC):
                            mm = nc.tensor.matmul(psG[:, h, :], xT[:, j.m2, c, :],
                                                  W[:, bass.ds(base + 1024 * c + 512 * h, 512)], start=(c == 0),
                                                  stop=(c == DC - 1))
                        mm.then_inc(s.gu_full, 1)

            def turn_h(l, s, j):
                if l.n == 0:
                    nc.tensor.transpose(psT[:, j.m2, 0:P], hh[:, j.m2, :], ident[:]).then_inc(s.hT_full, 1)
                else:
                    for h in range(2):
                        for f in range(4):
                            mm = nc.tensor.transpose(psG[:, 2 + h, f * P:(f + 1) * P],
                                                     h1g[:, (4 * h + f) * P:(4 * h + f + 1) * P], ident[:])
                        mm.then_inc(s.hT_full, 1)

            def down(l, s, j, rank):
                base = ring_at(l, rank)
                if l.n == 0:
                    nc.tensor.matmul(psO[:, j.m2, 0:D], hhT[:, j.m2, :], W[:, bass.ds(base + 512, 256)], start=True,
                                     stop=True).then_inc(s.y_full, 1)
                else:
                    for f in range(8):
                        mm = nc.tensor.matmul(psO[:, j.m2, 0:D], h1T[:, f * P:(f + 1) * P],
                                              W[:, bass.ds(base + 2048 + 256 * f, 256)], start=(f == 0), stop=(f == 7))
                    mm.then_inc(s.y_full, 1)

            route(L0E, S0)
            blocks(L0E, S0)

            def transpose_kv(b):
                pe.wait_ge(lat_ready, b + 1)
                for c in range(DC):
                    bank = bank_for_act() if c == 0 else bank_for_dve()
                    for i in range(NS):
                        nc.tensor.transpose(bank[:, i * SC:(i + 1) * SC], ctxn[:, i, c * P:(c + 1) * P],
                                            ident[0:SC, 0:SC])
                    nc.tensor.transpose(bank[:, S:KV], latn[:, c * P:(c + 1) * P],
                                        ident[0:T, 0:T]).then_inc(act_full if c == 0 else dve_full, 1)

            def keysL():
                for j in range(IC):
                    if j % 2 == 0:
                        keys_T(wkvL, 0, j, ctxT, KV, bank_for_act()).then_inc(act_full, 1)
                    else:
                        keys_T(wkvL, 0, j, ctxT, KV, bank_for_dve()).then_inc(dve_full, 1)

            def values_queriesL():
                for c, (k0, kn) in enumerate(chunks(KV, KC)):
                    values(wkvL, INNER, ctxT, k0, kn, 0, bank_for_act()).then_inc(act_full, 1)
                    values(wkvL, INNER, ctxT, k0, kn, 1, bank_for_dve()).then_inc(dve_full, 1)
                lat = ctxT[:, :, S:KV]
                project_T(wqL, lat, 0, 4, bank_for_act()).then_inc(act_full, 1)
                project_T(wqL, lat, 512, 4, bank_for_dve()).then_inc(dve_full, 1)

            pe.wait_ge(wL_in, 48)
            transpose_kv(0)
            evacuated()
            keysL()
            values_queriesL()
            transpose_kv(1)

            def batchL(b, more, more2):
                evacuated()
                attention(units2(), qT2, kT2, v2, KV, KC)
                if more:
                    keysL()
                transpose_out()
                evacuated()
                project_out(woL, oT, IC)
                if more:
                    values_queriesL()
                if more2:
                    transpose_kv(b + 2)

            with pe.Fori(0, B - 2) as b:
                act.enter(b, ACTL_JOBS)
                dve.enter(b, DVEL_JOBS)
                unit.enter(b, 16)
                ca.enter(b, 4)
                cd.enter(b, 12)
                oc.enter(b, 2)
                osbs.enter(b, 2)
                batchL(b, True, True)
            for t in (act, dve, unit, ca, cd, oc, osbs):
                t.leave(B - 2)
            batchL(B - 2, True, False)
            batchL(B - 1, False, False)
            route(L1E, S1)
            blocks(L1E, S1)

        @block.scalar
        def _(act):
            jobs, unit, pt = Tally(), Tally(), Tally()

            def filled():
                wait_apart(act, act_full, jobs.next())
                return psG[:, jobs.turn, :]

            def attention(units, keys, size):
                n = len(units)
                nb = len(chunks(keys, size)) if len(units[0]) == 1 else len(units[0])
                u0 = unit.now()
                for s in range(n + 2):
                    if s < n:
                        act.wait_ge(max_ready, u0 + s + 1)
                        for i, h in enumerate(units[s]):
                            e = nc.scalar.activation(probs[:, s % 4, i * keys:(i + 1) * keys],
                                                     psG[0:T, BANK[s % 4], i * keys:(i + 1) * keys], ACT.Exp,
                                                     bias=nmax[:, h:h + 1], accum_out=rsum[:, h:h + 1])
                        e.then_inc(probs_ready, 1)
                    u = s - 2
                    if 0 <= u and on_act(u):
                        act.wait_ge(probsT_ready, u0 + u + 1)
                        nc.scalar.activation(probsT[0:size, u % 2, 0:nb * T], psT[0:size, u % 2, 0:nb * T],
                                             ACT.Copy).then_inc(copied_act, 1)
                unit.next(n)

            def copy4(dst, scale=None):
                bank = filled()
                kw = {"scale": scale} if scale else {}
                nc.scalar.activation(dst, bank[:, 0:4 * T].rearrange("p (j t) -> p j t", j=4), ACT.Copy,
                                     **kw).then_inc(act_evac, 1)

            def affine(hT, n, b):
                bank = filled()
                for c in range(DC):
                    e = nc.scalar.activation(hT[:, c, :], bank[:, c * T:(c + 1) * T], ACT.Identity,
                                             bias=aff[:, 4 * n + 2 + c, bass.ds(b, 1)],
                                             scale=aff[:, 4 * n + c, bass.ds(b, 1)])
                e.then_inc(act_evac, 1)

            def qk1(b):
                affine(hT1, 0, b)
                copy4(qT1[:, 0:4, :], QSCALE)
                copy4(kT1[:, 0:4, :])

            def val1():
                bank = filled()
                nc.scalar.activation(v1[0:T, 0, 0:512], bank[0:T, :], ACT.Copy).then_inc(act_evac, 1)

            act.wait_ge(aff_done, 1)
            qk1(0)
            val1()

            def batch(b, last):
                attention(units1(), T, T)
                for j in range(0, IC, 2):
                    bank = filled()
                    nc.scalar.activation(kT2[:, j, 0:S], bank[:, 0:S], ACT.Copy).then_inc(act_evac, 1)
                copy4(oT[:, 0:4, :])
                for c in range(NS):
                    bank = filled()
                    nc.scalar.activation(v2[0:SC, c, 0:512], bank[0:SC, :], ACT.Copy).then_inc(act_evac, 1)
                affine(hT2, 1, b)
                copy4(qT2[:, 0:4, :], QSCALE)
                attention(units2(), S, SC)
                if not last:
                    qk1(b + 1)
                copy4(oT[:, 0:4, :])
                if not last:
                    val1()
                affine(hT2, 2, b)
                for half in range(2):
                    bank = filled()
                    for j in range(4):
                        f = 4 * half + j
                        e = nc.scalar.activation(gel[:, f, :], bank[:, j * T:(j + 1) * T], ACT.Gelu,
                                                 bias=cols[:, FB + FC + f:FB + FC + f + 1])
                    e.then_inc(act_evac, 1)

            with act.Fori(0, B - 1) as b:
                jobs.enter(b, ACT_JOBS)
                unit.enter(b, 20)
                batch(b, False)
            jobs.leave(B - 1)
            unit.leave(B - 1)
            batch(B - 1, True)

            def route(l, s):
                if l.n == 0:
                    for b in range(1, B + 2):
                        if b - 1 < B:
                            act.wait_ge(s.sh_gu, b)
                            nc.scalar.activation(sg[0:T, (b - 1) % 2, :], psG[0:T, 1 + (b - 1) % 2, 0:P],
                                                 ACT.Silu).then_inc(s.sh_sg, 1)
                        if b - 2 >= 0:
                            act.wait_ge(s.sh_hT, b - 1)
                            nc.scalar.activation(hhT[:, b % 2, 0:T], psG[:, 3, 0:T], ACT.Copy).then_inc(s.sh_hTc, 1)
                    for i in range(2):
                        act.wait_ge(s.logits_full, i + 1)
                        nc.scalar.activation(sc[:, 512 * i:512 * (i + 1)], psO[0:T, i, :],
                                             ACT.Sigmoid).then_inc(s.scores_ok, 1)
                else:
                    act.wait_ge(s.scores_ok, 1)
                    nc.scalar.activation(slotv[:, 0:B * l.E], slotv[:, 0:B * l.E], ACT.Exp).then_inc(s.exps, 1)

            def blocks(l, s):
                for i in range(4):
                    act.sem_inc(s.y_stored[i], 16)

                def step(turn, i, lo, hi):
                    j = At(turn, i - 2)
                    if lo >= 2:
                        if l.n == 0:
                            act.wait_ge(s.hT_full, j.j + 1)
                            nc.scalar.activation(hhT[:, j.m2, :], psT[:, j.m2, 0:P], ACT.Copy).then_inc(s.hT_done, 1)
                        else:
                            act.wait_ge(s.hT_full, 2 * j.j + 1)
                            nc.scalar.activation(h1T[:, 0:512], psG[:, 2, :], ACT.Copy).then_inc(s.hT_done, 1)
                    j = At(turn, i - 1)
                    if lo >= 1 and (hi or i < 1):
                        if l.n == 0:
                            act.wait_ge(s.gu_full, j.j + 1)
                            nc.scalar.activation(sg[:, j.m2, :], psG[:, 2 + j.m2, 0:P], ACT.Silu).then_inc(s.sg_done, 1)
                        else:
                            for h in range(2):
                                act.wait_ge(s.sg_done, 2 * j.j + h + 1)
                                if lo >= 2:
                                    act.wait_ge(s.hT_full, 2 * j.j)
                                e = nc.scalar.activation(h1g[:, 512 * h:512 * (h + 1)], h1b[:, 512 * h:512 * (h + 1)],
                                                         ACT.Gelu)
                            e.then_inc(s.h_done, 1)
                    j = At(turn, i - 2)
                    if lo >= 2:
                        act.wait_ge(s.y_full, j.j + 2)
                        act.wait_ge(s.y_stored[j.m], 16 * j.turn + 16)
                        if l.n == 0:
                            nc.scalar.activation(ysb[:, j.m, :], psO[:, j.m2, 0:D], ACT.Copy).then_inc(s.y_done, 1)
                        act.wait_ge(s.y_done, j.j + 1)
                        act.dma_start(ydram[l.n].rearrange("(j p) d -> j p d", p=P)[bass.ds(j.j, 1)].rearrange("o p d -> (o p) d"),
                                      ysb[:, j.m, :]).then_inc(s.y_stored[j.m], 16)

                for i in range(4):
                    step(0, i, i, True)
                with act.Fori(1, l.NBLK // 4) as turn:
                    for i in range(4):
                        step(turn, i, 4, True)
                for i in range(2):
                    step(l.NBLK // 4, i, 4, False)

            route(L0E, S0)
            blocks(L0E, S0)

            def copy_kv(b):
                bank = filled()
                nc.scalar.activation(ctxT[:, 0, 0:S], bank[:, 0:S], ACT.Identity, bias=cols[:, LN1B:LN1B + 1],
                                     scale=cols[:, LN1W:LN1W + 1])
                nc.scalar.activation(ctxT[:, 0, S:KV], bank[:, S:KV], ACT.Identity,
                                     bias=affL[:, 2, bass.ds(b, 1)],
                                     scale=affL[:, 0, bass.ds(b, 1)]).then_inc(act_evac, 1)

            def keysL():
                for j in range(0, IC, 2):
                    bank = filled()
                    nc.scalar.activation(kT2[:, j, :], bank[:, 0:KV], ACT.Copy).then_inc(act_evac, 1)

            def values_queriesL():
                for c, (k0, kn) in enumerate(chunks(KV, KC)):
                    bank = filled()
                    nc.scalar.activation(v2[0:kn, c, 0:512], bank[0:kn, :], ACT.Copy).then_inc(act_evac, 1)
                copy4(qT2[:, 0:4, :], QSCALE)

            copy_kv(0)
            keysL()
            values_queriesL()
            copy_kv(1)

            def batchL(b, more, more2):
                attention(units2(), KV, KC)
                if more:
                    keysL()
                copy4(oT[:, 0:4, :])
                if more:
                    values_queriesL()
                if more2:
                    copy_kv(b + 2)

            with act.Fori(0, B - 2) as b:
                jobs.enter(b, ACTL_JOBS)
                unit.enter(b, 16)
                batchL(b, True, True)
            jobs.leave(B - 2)
            unit.leave(B - 2)
            batchL(B - 2, True, False)
            batchL(B - 1, False, False)
            route(L1E, S1)
            blocks(L1E, S1)

        @block.vector
        def _(dve):
            jobs, unit, step, halves, gels = Tally(), Tally(), Tally(), Tally(), Tally()

            def chain(ins):
                ins.then_inc(dve_step, 1)
                wait_apart(dve, dve_step, step.next())

            def filled():
                dve.wait_ge(dve_full, jobs.next())
                return psG[:, 2 + jobs.turn, :]

            def rsqrt(y, var, t, v):
                inverse_root(nc.vector, chain, y, var, t, v)

            def layernorm(dst, src, p):
                chain(nc.vector.bn_stats(st[0:p, 0, :], src))
                chain(nc.vector.bn_aggr(mv[0:p, 0, :], st[0:p, 0, :]))
                rsqrt(ry[0:p, 0:1], mv[0:p, 0, 1:2], rt[0:p, 0:1], ve[0:p, 0:1])
                return nc.vector.tensor_scalar(dst, src, mv[0:p, 0, 0:1], ry[0:p, 0:1], ALU.subtract, ALU.mult)

            nc.vector.memset(psT[:], 0.0)
            dve.wait_ge(consts, 8)
            nc.vector.tensor_copy(iotaf[:], iotai[:])
            dve.wait_ge(x_in, 16)

            def all_stats(src, mu, rs):
                for b in range(B):
                    chain(nc.vector.bn_stats(st[0:T, b, :], src(b)))
                    chain(nc.vector.bn_aggr(mv[0:T, b, :], st[0:T, b, :]))
                chain(nc.vector.tensor_copy(mu[:], mv[0:T, :, 0]))
                rsqrt(rs[:], mv[0:T, :, 1], rt[0:T, :], ve[0:T, :])

            all_stats(lambda b: X[:, b, :], mu1, rs1)

            def normed(b):
                chain(nc.vector.tensor_scalar(hn2[:], X[:, b, :], mu1[:, b:b + 1], rs1[:, b:b + 1], ALU.subtract,
                                              ALU.mult))
                return hn2[:]

            all_stats(normed, mu2, rs2)
            nc.vector.tensor_copy(mv[0:T, 0, 0:1], mu2[:, 0:1]).then_inc(stats_done, 1)
            dve.wait_ge(small_in, 96)
            bank = filled()
            chain(nc.vector.tensor_tensor(aff[:], bank[:, 0:12 * B].rearrange("p (j b) -> p j b", b=B),
                                          cols[:, NB:NB + 12].unsqueeze(2).broadcast_to([P, 12, B]), ALU.add))
            lw, lb = (cols[:, k:k + 2].unsqueeze(2).broadcast_to([P, DC, B]) for k in (LN2W, LN2B))
            for k, v in ((0, lw), (2, lb)):
                chain(nc.vector.scalar_tensor_tensor(affL[:, k:k + 2, :], condT[:], 1.0, v, ALU.add, ALU.mult))
            chain(nc.vector.tensor_tensor(affL[:, 2:4, :], affL[:, 2:4, :], condT[:], ALU.add))
            for n in range(3):
                e = nc.vector.tensor_scalar(aff[:, 4 * n:4 * n + 2, :], aff[:, 4 * n:4 * n + 2, :], 1.0, None, ALU.add)
                if n < 2:
                    chain(e)
            e.then_inc(aff_done, 1)
            dve.wait_ge(aff_done, 1)
            nc.vector.tensor_copy(st[:, 0, 0:1], aff[:, 0, 0:1]).then_inc(dve_evac, 1)

            def attention(units, keys, size, between=None):
                n = len(units)
                nb = len(chunks(keys, size)) if len(units[0]) == 1 else len(units[0])
                u0 = unit.now()

                def normalise(half):
                    dve.wait_ge(outputs_ready, halves.next())
                    chain(nc.vector.reciprocal(rinv[:, 8 * half:8 * half + 8], rsum[:, 8 * half:8 * half + 8]))
                    nc.vector.tensor_tensor(
                        osb[:, 512 * half:512 * (half + 1)].rearrange("t (h d) -> t h d", h=8),
                        psO[0:T, half, :].rearrange("t (h d) -> t h d", h=8),
                        rinv[:, 8 * half:8 * half + 8].unsqueeze(2).broadcast_to([T, 8, DH]),
                        ALU.mult).then_inc(osb_ready, 1)

                for s in range(n + 2):
                    if s < n:
                        hs = units[s]
                        dve.wait_ge(scores_ready, u0 + s + 1)
                        nc.vector.tensor_reduce(nmax[:, hs[0]:hs[-1] + 1:2] if len(hs) > 1 else nmax[:, hs[0]:hs[0] + 1],
                                                psG[0:T, BANK[s % 4], 0:len(hs) * keys].rearrange(
                                                    "t (h k) -> t h k", h=len(hs)),
                                                AXX, ALU.max, negate=True).then_inc(max_ready, 1)
                    u = s - 2
                    if 0 <= u and not on_act(u):
                        dve.wait_ge(probsT_ready, u0 + u + 1)
                        nc.vector.tensor_copy(probsT[0:size, u % 2, 0:nb * T],
                                              psT[0:size, u % 2, 0:nb * T]).then_inc(copied_dve, 1)
                    if s == n // 2 + 3:
                        normalise(0)
                    if between:
                        between(s)
                normalise(1)
                unit.next(n)

            def copy4(dst, scale=None):
                bank = filled()
                src = bank[:, 0:4 * T].rearrange("p (j t) -> p j t", j=4)
                if scale:
                    nc.vector.tensor_scalar(dst, src, scale, None, ALU.mult).then_inc(dve_evac, 1)
                else:
                    nc.vector.tensor_copy(dst, src).then_inc(dve_evac, 1)

            def qk1():
                copy4(qT1[:, 4:8, :], QSCALE)
                copy4(kT1[:, 4:8, :])

            def val1():
                bank = filled()
                nc.vector.tensor_copy(v1[0:T, 0, 512:1024], bank[0:T, :]).then_inc(dve_evac, 1)

            qk1()
            val1()

            def batch(b, last):
                attention(units1(), T, T)
                for j in range(1, IC, 2):
                    bank = filled()
                    nc.vector.tensor_copy(kT2[:, j, 0:S], bank[:, 0:S]).then_inc(dve_evac, 1)
                copy4(oT[:, 4:8, :])
                bank = filled()
                dve.wait_ge(hn1_ready, b + 1)
                nc.vector.tensor_tensor(R1[:], bank[0:T, 0:D], xnb[:], ALU.add).then_inc(dve_evac, 1)
                wait_apart(dve, dve_evac, jobs.now())
                layernorm(hn2[:], R1[:], T).then_inc(hn2_ready, 1)
                for c in range(NS):
                    bank = filled()
                    nc.vector.tensor_copy(v2[0:SC, c, 512:1024], bank[0:SC, :]).then_inc(dve_evac, 1)
                copy4(qT2[:, 4:8, :], QSCALE)
                attention(units2(), S, SC)
                if not last:
                    qk1()
                copy4(oT[:, 4:8, :])
                bank = filled()
                dve.wait_ge(r1b_ready, b + 1)
                nc.vector.tensor_tensor(R2[:], bank[0:T, 0:D], R1b[:], ALU.add).then_inc(dve_evac, 1)
                wait_apart(dve, dve_evac, jobs.now())
                layernorm(hn2[:], R2[:], T).then_inc(hn2_ready, 1)
                if not last:
                    val1()
                for half in range(2):
                    bank = filled()
                    dve.wait_ge(act_evac, gels.next())
                    for j in range(4):
                        f = 4 * half + j
                        e = nc.vector.scalar_tensor_tensor(uT[:, f, :], bank[:, j * T:(j + 1) * T],
                                                           cols[:, FB + f:FB + f + 1], gel[:, f, :], ALU.add, ALU.mult)
                    e.then_inc(dve_evac, 1)
                bank = filled()
                dve.wait_ge(r2b_ready, b + 1)
                nc.vector.tensor_tensor(X[:, bass.ds(b, 1), :].rearrange("t o d -> t (o d)"), bank[0:T, 0:D], R2b[:],
                                        ALU.add).then_inc(dve_evac, 1)

            with dve.Fori(0, B - 1) as b:
                jobs.enter(b, DVE_JOBS)
                unit.enter(b, 20)
                step.enter(b, 36)
                halves.enter(b, 4)
                gels.base = 4 + ACT_JOBS * b + 16
                gels.k = 0
                batch(b, False)
            for t in (jobs, unit, step, halves):
                t.leave(B - 1)
            gels.base, gels.k = 4 + ACT_JOBS * (B - 1) + 12, 0
            batch(B - 1, True)

            def route(l, s):
                E, K = l.E, l.K
                BE = B * E
                wait_apart(dve, dve_evac, jobs.now())
                for b in range(B):
                    e = nc.vector.bn_stats(st[0:T, b, :], X[:, b, :])
                chain(e)
                for b in range(B):
                    e = nc.vector.bn_aggr(mv[0:T, b, :], st[0:T, b, :])
                chain(e)
                rsqrt(rs1[:], mv[0:T, :, 1], rt[0:T, :], ve[0:T, :])
                for b in range(B):
                    nc.vector.tensor_scalar(hall[:, b, :], X[:, b, :], mv[0:T, b, 0:1], rs1[:, b:b + 1], ALU.subtract,
                                            ALU.mult).then_inc(s.normed, 1)
                for b in range(B + 3):
                    if b < B:
                        dve.wait_ge(s.route_a, b + 1)
                        nc.vector.tensor_copy(hTr[:, b % 4], psG[:, 0, 0:DC * T].rearrange(
                            "p (c t) -> p c t", c=DC)).then_inc(s.hT_ready, 1)
                    if l.n == 0 and 0 <= b - 1 < B:
                        dve.wait_ge(s.sh_sg, b)
                        nc.vector.tensor_tensor(hh[0:T, (b - 1) % 2, :], sg[0:T, (b - 1) % 2, :],
                                                psG[0:T, 1 + (b - 1) % 2, P:2 * P], ALU.mult).then_inc(s.sh_h, 1)
                    if l.n == 0 and 0 <= b - 3:
                        dve.wait_ge(s.sh_y, b - 2)
                        nc.vector.tensor_tensor(X[:, b - 3, :], psT[0:T, (b - 3) % 2, 0:D], X[:, b - 3, :],
                                                ALU.add).then_inc(s.sh_done, 1)
                if l.n == 0:
                    dve.wait_ge(s.sh_done, B)
                v3 = lambda v: v[:, 0:BE].rearrange("t (b e) -> t b e", b=B)
                if l.n == 0:
                    dve.wait_ge(s.scores_ok, 2)
                    scores = sc
                else:
                    dve.wait_ge(s.logits_full, 1)
                    chain(nc.vector.tensor_tensor(v3(sc), v3(psO[0:T, 0, :]), br[:].unsqueeze(1).broadcast_to([T, B, E]),
                                                  ALU.add))
                    scores = sc
                for b in range(B):
                    e = nc.vector.max(top[:, b, :], scores[:, b * E:(b + 1) * E])
                chain(e)
                for b in range(B):
                    e = nc.vector.max_index(topi[:, b, :], top[:, b, :], scores[:, b * E:(b + 1) * E])
                chain(e)
                chain(nc.vector.tensor_copy(topf[:], topi[:]))
                if l.n == 0:
                    for b in range(B):
                        e = nc.vector.match_replace(rep_[:, b * E:(b + 1) * E], top[:, b, :], scores[:, b * E:(b + 1) * E],
                                                    -1.0)
                    chain(e)
                    chain(nc.vector.tensor_scalar(msk[:, 0:BE], rep_[:, 0:BE], -1.0, None, ALU.is_equal))
                else:
                    chain(nc.vector.tensor_tensor(v3(msk), iotaf[0:T, 0:E].unsqueeze(1).broadcast_to([T, B, E]),
                                                  topf[:, :, 0:1].broadcast_to([T, B, E]), ALU.is_equal))
                chain(nc.vector.memset(cum[:, 0:E], 0.0))
                for b in range(B):
                    e = nc.vector.tensor_tensor(cum[:, (b + 1) * E:(b + 2) * E], cum[:, b * E:(b + 1) * E],
                                                msk[:, b * E:(b + 1) * E], ALU.add)
                    if b < B - 1:
                        chain(e)
                e.then_inc(s.mask_ok, 1)
                if l.n == 0:
                    chain(nc.vector.tensor_reduce(rs1[:], top[:], AXX, ALU.add))
                    chain(nc.vector.tensor_scalar(rs1[:], rs1[:], 1e-9, None, ALU.add))
                    chain(nc.vector.reciprocal(rs1[:], rs1[:]))
                    chain(nc.vector.tensor_tensor(wgt[:], top[:], rs1[:].unsqueeze(2).broadcast_to([T, B, K]), ALU.mult))
                else:
                    nc.vector.tensor_tensor(v3(slotv), v3(sc), top[:, :, 0:1].broadcast_to([T, B, E]),
                                            ALU.subtract).then_inc(s.scores_ok, 1)
                    dve.wait_ge(s.exps, 1)
                    chain(nc.vector.tensor_reduce(rs1[:], v3(slotv), AXX, ALU.add))
                    chain(nc.vector.reciprocal(wgt[:, :, 0], rs1[:]))
                dve.wait_ge(s.counts_full, 1)
                chain(nc.vector.tensor_scalar(ecoli[0:E, :], psG[0:E, 0, 0:1], float(P - 1), None, ALU.add))
                chain(nc.vector.tensor_scalar(ecoli[0:E, :], ecoli[0:E, :], 7, None, ALU.arith_shift_right))
                chain(nc.vector.tensor_copy(ecol[0:E, 1:2], ecoli[0:E, :]))
                chain(nc.vector.tensor_scalar(ecol[0:E, 2:3], ecol[0:E, 1:2], 0.0, None, ALU.is_gt))
                nc.vector.tensor_scalar(bmat[0:E, :], ones[0:E, :], ecol[0:E, 1:2], None,
                                        ALU.mult).then_inc(s.blocks_ok, 1)
                dve.wait_ge(s.incl_full, 1)
                chain(nc.vector.tensor_copy(ecol[0:E, 3:5], psG[0:E, 1, 64:66]))
                chain(nc.vector.tensor_tensor(ecol[0:E, 5:6], ecol[0:E, 4:5], ecol[0:E, 2:3], ALU.subtract))
                nc.vector.tensor_scalar(gmat[0:E, 0:l.NBLK], iotaf[0:E, 0:l.NBLK], ecol[0:E, 3:4], None, ALU.is_ge)
                nc.vector.tensor_scalar(gmat[0:E, l.NBLK:l.NBLK + E], iotaf[0:E, 0:E], ecol[0:E, 4:5], None, ALU.is_ge)
                nc.vector.tensor_scalar(gmat[0:E, l.NBLK + E:l.NBLK + 2 * E], iotaf[0:E, 0:E], ecol[0:E, 5:6], None,
                                        ALU.is_ge).then_inc(s.incl_ok, 1)
                chain(nc.vector.tensor_scalar(startS[:, 0:E], psG[0:T, 1, 0:E], float(P), None, ALU.mult))
                dve.wait_ge(s.rows_full, 1)
                nc.vector.tensor_scalar(brow[0:1, 0:l.NBLK], psG[0:1, 2, 0:l.NBLK], float(E - 1), None, ALU.min)
                nc.vector.tensor_scalar(rrow[0:1, 0:E], psG[0:1, 2, 256:256 + E], float(E - 1), None, ALU.min)
                nc.vector.tensor_copy(lrow[0:1, 0:E], psG[0:1, 2, 320:320 + E]).then_inc(s.tables, 1)
                dve.wait_ge(s.ranks_full, 1)
                per = 8 if l.n == 0 else 16
                for i in range(B // per):
                    e = nc.vector.tensor_tensor(v3(slotv)[:, i * per:(i + 1) * per, :],
                                                psO[0:T, i, 0:per * E].rearrange("t (b e) -> t b e", b=per),
                                                startS[:, 0:E].unsqueeze(1).broadcast_to([T, per, E]), ALU.add)
                chain(e)
                for b in range(B):
                    for k in range(K):
                        e = nc.vector.scalar_tensor_tensor(tmpv[:, 0:E], iotaf[0:T, 0:E], topf[:, b, k:k + 1],
                                                           slotv[:, b * E:(b + 1) * E], ALU.is_equal, ALU.mult,
                                                           accum_out=slotf[:, b, k:k + 1])
                        chain(e)
                chain(nc.vector.tensor_copy(sloti[:, :, 0:K], slotf[:, :, 0:K]))
                chain(nc.vector.tensor_scalar(slotj[:, :, 0:K], sloti[:, :, 0:K], 7, None, ALU.arith_shift_right))
                chain(nc.vector.tensor_scalar(slotf[:, :, 0:K], slotf[:, :, 0:K], float(l.NBLK), None, ALU.mult))
                nc.vector.scalar_tensor_tensor(desti[:, :, 0:K], slotj[:, :, 0:K], -float(P * l.NBLK - 1),
                                               slotf[:, :, 0:K], ALU.mult, ALU.add).then_inc(s.slots_ok, 1)

            def blocks(l, s):
                def step(turn, i, lo, hi, ranks):
                    j = At(turn, i)
                    if hi:
                        dve.wait_ge(s.xT_full, j.j + 1)
                        src = psG[:, j.m2, 0:DC * P] if l.n == 0 else psT[:, 0, 0:DC * P]
                        nc.vector.tensor_copy(xT[:, j.m2], src.rearrange("p (c t) -> p c t", c=DC)).then_inc(s.xT_done, 1)
                    j = At(turn, i - 2)
                    if l.n == 1 and lo >= 2:
                        dve.wait_ge(s.hT_full, 2 * j.j + 2)
                        nc.vector.tensor_copy(h1T[:, 512:1024], psG[:, 3, :]).then_inc(s.hT_done2, 1)
                    j = At(turn, i - 1)
                    if lo >= 1 and (hi or i < 1):
                        if l.n == 0:
                            dve.wait_ge(s.sg_done, j.j + 1)
                            nc.vector.tensor_tensor(hh[:, j.m2, :], sg[:, j.m2, :], psG[:, 2 + j.m2, P:2 * P],
                                                    ALU.mult).then_inc(s.h_done, 1)
                        else:
                            for h in range(2):
                                rank = ranks[i + 1]
                                dve.wait_ge(s.gu_full, 2 * j.j + h + 1)
                                if lo >= 2:
                                    dve.wait_ge(s.h_done, j.j)
                                nc.vector.tensor_tensor(
                                    h1b[:, 512 * h:512 * (h + 1)], psG[:, h, :],
                                    W[:, bass.ds(RING + (rank % l.R) * l.wsize + 4096 + 512 * h, 512)],
                                    ALU.add).then_inc(s.sg_done, 1)
                    j = At(turn, i - 2)
                    if l.n == 1 and lo >= 2:
                        rank = ranks[i]
                        dve.wait_ge(s.y_full, j.j + 2)
                        dve.wait_ge(s.y_stored[j.m], 16 * j.turn + 16)
                        nc.vector.tensor_tensor(ysb[:, j.m, :], psO[:, j.m2, 0:D],
                                                W[:, bass.ds(RING + (rank % l.R) * l.wsize + 5120, 256)],
                                                ALU.add).then_inc(s.y_done, 1)

                use = l.n == 1
                ranks = (0, 0) + tuple(ranks_of(DVE, l, 0, 4)) if use else None
                for i in range(4):
                    step(0, i, i, True, ranks)
                with dve.Fori(1, l.NBLK // 4) as turn:
                    ranks = ranks_of(DVE, l, 4 * turn - 2, 6) if use else None
                    for i in range(4):
                        step(turn, i, 4, True, ranks)
                ranks = ranks_of(DVE, l, l.NBLK - 2, 2) if use else None
                for i in range(2):
                    step(l.NBLK // 4, i, 4, False, ranks)

            def add_rows(b, k):
                if k == 0:
                    wait_apart(dve, S0.yk_in[0], 16 * L0E.K * (b + 1))
                else:
                    wait_apart(dve, dve_step, step.now())
                xb = X[:, bass.ds(b, 1), :].rearrange("t o d -> t (o d)")
                e = nc.vector.scalar_tensor_tensor(xb, yk[:, k, :],
                                                   wgt[:, bass.ds(b, 1), k:k + 1].rearrange("t o k -> t (o k)"),
                                                   xb, ALU.mult, ALU.add)
                if k < L0E.K - 1:
                    e.then_inc(dve_step, 1)
                    step.next()
                else:
                    e.then_inc(S0.combined, 1)

            def combine1():
                def tile(turn, u):
                    b = 2 * turn + u
                    dve.wait_ge(S1.yk_in[u], 16 * (turn + 1))
                    xb = X[:, bass.ds(b, 1), :].rearrange("t o d -> t (o d)")
                    nc.vector.scalar_tensor_tensor(xb, yk[:, u, :], wgt[:, bass.ds(b, 1), 0:1].rearrange("t o k -> t (o k)"),
                                                   xb, ALU.mult, ALU.add).then_inc(S1.combined, 1)

                with dve.Fori(0, B // 2) as turn:
                    tile(turn, 0)
                    tile(turn, 1)

            route(L0E, S0)
            blocks(L0E, S0)

            def measure_rows(b):
                one = bass.ds(b, 1)
                xb = X[:, one, :].rearrange("t o d -> t (o d)")
                dve.wait_ge(ctxr_in, 16 * b + 16)
                for c in range(NS):
                    nc.vector.bn_stats(cst[0:SC, c, :], ctxr[:, c, :])
                wait_apart(dve, S0.combined, b + 1)
                chain(nc.vector.bn_stats(cst[0:T, 3, :], xb))
                for c in range(NS):
                    nc.vector.bn_aggr(cmv[0:SC, c, :], cst[0:SC, c, :])
                nc.vector.bn_aggr(cmv[0:T, 3, :], cst[0:T, 3, :]).then_inc(lat_stats, 1)

            def ahead(b):
                def at(s):
                    if s < L0E.K:
                        add_rows(b, s)
                    if s == L0E.K + 1:
                        measure_rows(b)
                return at

            def copy_kv(b):
                bank = filled()
                nc.vector.tensor_scalar(ctxT[:, 1, 0:S], bank[:, 0:S], cols[:, LN1W + 1:LN1W + 2],
                                        cols[:, LN1B + 1:LN1B + 2], ALU.mult, ALU.add)
                nc.vector.tensor_scalar(ctxT[:, 1, S:KV], bank[:, S:KV], affL[:, 1, bass.ds(b, 1)],
                                        affL[:, 3, bass.ds(b, 1)], ALU.mult, ALU.add).then_inc(dve_evac, 1)

            def keysL():
                for j in range(1, IC, 2):
                    bank = filled()
                    nc.vector.tensor_copy(kT2[:, j, :], bank[:, 0:KV]).then_inc(dve_evac, 1)

            def values_queriesL():
                for c, (k0, kn) in enumerate(chunks(KV, KC)):
                    bank = filled()
                    nc.vector.tensor_copy(v2[0:kn, c, 512:1024], bank[0:kn, :]).then_inc(dve_evac, 1)
                copy4(qT2[:, 4:8, :], QSCALE)

            chain(nc.vector.memset(cmv[:], 0.0))
            for k in range(L0E.K):
                add_rows(0, k)
            measure_rows(0)
            copy_kv(0)
            keysL()
            for k in range(L0E.K):
                add_rows(1, k)
            measure_rows(1)
            values_queriesL()
            copy_kv(1)

            def batchL(b, more, more2):
                attention(units2(), KV, KC, ahead(b + 2) if more2 else None)
                if more:
                    keysL()
                copy4(oT[:, 4:8, :])
                bank = filled()
                xb = X[:, bass.ds(b, 1), :].rearrange("t o d -> t (o d)")
                nc.vector.tensor_tensor(xb, bank[0:T, 0:D], xb, ALU.add).then_inc(dve_evac, 1)
                if more:
                    values_queriesL()
                if more2:
                    copy_kv(b + 2)

            with dve.Fori(0, B - 2) as b:
                jobs.enter(b, DVEL_JOBS)
                unit.enter(b, 16)
                step.enter(b, 10)
                halves.enter(b, 2)
                batchL(b, True, True)
            for t in (jobs, unit, step, halves):
                t.leave(B - 2)
            batchL(B - 2, True, False)
            batchL(B - 1, False, False)
            dve.wait_ge(dve_evac, jobs.now())
            nc.vector.memset(cry[:], 0.0).then_inc(x3_done, B)
            route(L1E, S1)
            blocks(L1E, S1)
            combine1()


def kernel(**inputs):
    import numpy as np
    import concourse.bacc as bacc
    from concourse.bass_utils import run_bass_kernel_spmd as run

    g = {k: np.asarray(v) for k, v in inputs.items()}

    def columns(v):
        return v.reshape(-1, 128).T

    L0, L1 = "L0_xcond_", "L1_xcond_"
    ar = {
        "x": g["x"],
        "condT": g["cond_1024"].T,
        "ctx": g["ctx_1024"],
        "ctxT": g["ctx_1024"].transpose(0, 2, 1),
        "cols": np.concatenate([columns(g[L0 + "norm1_b"]), columns(g[L0 + "norm2_b"]), columns(g[L0 + "norm3_b"]),
                                columns(g[L0 + "ff_b1"]), columns(g[L1 + "ln1_w"]), columns(g[L1 + "ln1_b"]),
                                columns(g[L1 + "ln2_w"]), columns(g[L1 + "ln2_b"]),
                                columns(g["L1_ffn_b1"].reshape(-1))], 1),
        "rows": np.stack([g[L0 + "attn1_bo"], g[L0 + "attn2_bo"], g[L0 + "ff_b2"]]),
        "nw": np.stack([g[L0 + "norm1_w"], g[L0 + "norm2_w"], g[L0 + "norm3_w"]]),
        "wq1": g[L0 + "attn1_wq"], "wk1": g[L0 + "attn1_wk"], "wv1": g[L0 + "attn1_wv"], "wo1": g[L0 + "attn1_wo"],
        "wq2": g[L0 + "attn2_wq"], "wk2": g[L0 + "attn2_wk"], "wv2": g[L0 + "attn2_wv"], "wo2": g[L0 + "attn2_wo"],
        "wqL": g[L1 + "Wq"].T, "wkvL": g[L1 + "Wkv"].T, "woL": g[L1 + "Wo"].T,
        "rw0": g["L0_ffn_router_w"], "rw1": g["L1_ffn_Wr"], "br": g["L1_ffn_br"],
        "ew0": np.concatenate([
            np.concatenate([g["L0_ffn_expert_gate_k"], g["L0_ffn_expert_up_k"]], 2).reshape(64, 2, 128, 256)
            .transpose(0, 2, 1, 3).reshape(64, 128, 512), g["L0_ffn_expert_down_k"]], 2),
        "ew1": np.concatenate([
            g["L1_ffn_W1"].reshape(8, 2, 128, 1024).transpose(0, 2, 1, 3).reshape(8, 128, 2048),
            g["L1_ffn_W2"].reshape(8, 8, 128, 256).transpose(0, 2, 1, 3).reshape(8, 128, 2048)], 2),
        "eb1": np.concatenate([g["L1_ffn_b1"], g["L1_ffn_b2"]], 1),
        "shw": np.concatenate([
            np.concatenate([g["L0_ffn_shared_gate_w"], g["L0_ffn_shared_up_w"]], 1).reshape(2, 128, 256)
            .transpose(1, 0, 2).reshape(128, 512), g["L0_ffn_shared_down_w"]], 1),
        "fw1": g[L0 + "ff_w1"], "fw2": g[L0 + "ff_w2"],
    }
    ar = {"in_" + k: np.ascontiguousarray(v) for k, v in ar.items()}
    nc = bacc.Bacc("TRN2", target_bir_lowering=False, num_devices=1)
    aps = {k[3:]: nc.dram_tensor(k, v.shape, mybir.dt.from_np(v.dtype), kind="ExternalInput").ap()
           for k, v in ar.items()}
    out = nc.dram_tensor("out_0", (B, T, D), F32, kind="ExternalOutput").ap()
    build(nc, aps, out)
    r = run(nc, [ar], core_ids=[0])
    return r.results[0]["out_0"]
```
